# Optimizing a Trainium2 kernel written in Bass

```python
import numpy as np
import jax
import jax.numpy as jnp

def _softmax(x, axis=-1):
    return jax.nn.softmax(x, axis=axis)

def _gelu(x):
    return jax.nn.gelu(x, approximate=True)

def _silu(x):
    return jax.nn.silu(x)

def _sigmoid(x):
    return jax.nn.sigmoid(x)

def _layernorm(x, axis=-1, eps=1e-05):
    m = jnp.mean(x, axis=axis, keepdims=True)
    v = jnp.var(x, axis=axis, keepdims=True)
    return (x - m) / jnp.sqrt(v + eps)

def _scatter_add(tgt, idx, src, axis=0):
    return tgt.at[idx].add(src)

def _segment_sum(src, seg, n):
    return jax.ops.segment_sum(src, seg, n)
kernel_name = 'mk_macaron_d1_jaxref_r8_c31123'

def setup_inputs(seed: int=0):
    np.random.seed(seed)
    _w = jnp.asarray

    def _L0_attn_setup():
        import jax, jax.numpy as jnp
        import numpy as np
        HIDDEN = 128
        HEADS = 16
        HEAD_DIM = HIDDEN // HEADS
        key = jax.random.key(seed)
        ks = jax.random.split(key, 9)
        s = 1.0 / np.sqrt(HIDDEN)

        def lin(kw, kb):
            W = jax.random.uniform(kw, (HIDDEN, HIDDEN), jnp.float32, -s, s)
            b = jax.random.uniform(kb, (HIDDEN,), jnp.float32, -s, s)
            return (W, b)
        Wq, bq = lin(ks[0], ks[1])
        Wk, bk = lin(ks[2], ks[3])
        Wv, bv = lin(ks[4], ks[5])
        Wo, bo = lin(ks[6], ks[7])
        x = jax.random.normal(ks[8], (2, 256, HIDDEN), jnp.float32)
        return {'x': x, 'Wq': Wq, 'bq': bq, 'Wk': Wk, 'bk': bk, 'Wv': Wv, 'bv': bv, 'Wo': Wo, 'bo': bo}
    _L0_attn_in = _L0_attn_setup()

    def _L0_ffn_setup():
        import jax, jax.numpy as jnp
        import numpy as np
        K = 2
        key = jax.random.key(seed)
        ks = jax.random.split(key, 7)
        B, S, D, E = (2, 256, 128, 8)
        H = 4 * D
        sd = 1.0 / np.sqrt(D)
        sh = 1.0 / np.sqrt(H)
        return {'x': jax.random.normal(ks[0], (B, S, D), jnp.float32), 'Wr': jax.random.normal(ks[1], (D, E), jnp.float32) * sd, 'br': jax.random.normal(ks[2], (E,), jnp.float32) * sd, 'W1': jax.random.normal(ks[3], (E, D, H), jnp.float32) * sd, 'b1': jax.random.normal(ks[4], (E, H), jnp.float32) * sd, 'W2': jax.random.normal(ks[5], (E, H, D), jnp.float32) * sh, 'b2': jax.random.normal(ks[6], (E, D), jnp.float32) * sh}
    _L0_ffn_in = _L0_ffn_setup()
    _d = {'L0_attn_x': _L0_attn_in['x'], 'L0_attn_Wq': _L0_attn_in['Wq'], 'L0_attn_bq': _L0_attn_in['bq'], 'L0_attn_Wk': _L0_attn_in['Wk'], 'L0_attn_bk': _L0_attn_in['bk'], 'L0_attn_Wv': _L0_attn_in['Wv'], 'L0_attn_bv': _L0_attn_in['bv'], 'L0_attn_Wo': _L0_attn_in['Wo'], 'L0_attn_bo': _L0_attn_in['bo'], 'L0_ffn_Wr': _L0_ffn_in['Wr'], 'L0_ffn_br': _L0_ffn_in['br'], 'L0_ffn_W1': _L0_ffn_in['W1'], 'L0_ffn_b1': _L0_ffn_in['b1'], 'L0_ffn_W2': _L0_ffn_in['W2'], 'L0_ffn_b2': _L0_ffn_in['b2']}
    _x0 = _d['L0_attn_x']
    _d['L0_attn_x'] = jax.random.normal(jax.random.fold_in(jax.random.key(seed), 1), (8, 512, 128), dtype=_x0.dtype)
    del _x0
    return _d

def reference(L0_attn_x, L0_attn_Wq, L0_attn_bq, L0_attn_Wk, L0_attn_bk, L0_attn_Wv, L0_attn_bv, L0_attn_Wo, L0_attn_bo, L0_ffn_Wr, L0_ffn_br, L0_ffn_W1, L0_ffn_b1, L0_ffn_W2, L0_ffn_b2):

    def _L0_attn_ref(x, Wq, bq, Wk, bk, Wv, bv, Wo, bo):
        import jax, jax.numpy as jnp
        import numpy as np
        HIDDEN = 128
        HEADS = 16
        HEAD_DIM = HIDDEN // HEADS
        B, S, _ = x.shape

        def proj(W, b):
            y = jnp.einsum('bsh,oh->bso', x, W) + b
            return y.reshape(B, S, HEADS, HEAD_DIM)
        q = proj(Wq, bq)
        k = proj(Wk, bk)
        v = proj(Wv, bv)
        scale = 1.0 / np.sqrt(HEAD_DIM)
        scores = jnp.einsum('bqhd,bkhd->bhqk', q, k) * scale
        probs = jax.nn.softmax(scores, axis=-1)
        out = jnp.einsum('bhqk,bkhd->bqhd', probs, v).reshape(B, S, HIDDEN)
        return jnp.einsum('bsh,oh->bso', out, Wo) + bo

    def _L0_ffn_ref(x, Wr, br, W1, b1, W2, b2):
        import jax, jax.numpy as jnp
        import numpy as np
        K = 2
        E = Wr.shape[-1]
        scores = jnp.einsum('bsd,de->bse', x, Wr) + br
        _, topk_idx = jax.lax.top_k(scores, K)
        indicator = jax.nn.one_hot(topk_idx, E, dtype=scores.dtype).sum(-2)
        neg_inf = jnp.asarray(-jnp.inf, scores.dtype)
        weights = jax.nn.softmax(jnp.where(indicator > 0, scores, neg_inf), axis=-1)
        out = jnp.zeros_like(x)
        for i in range(E):
            xi = x * indicator[..., i:i + 1]
            h = jax.nn.relu(jnp.einsum('bsd,dh->bsh', xi, W1[i]) + b1[i])
            yi = jnp.einsum('bsh,hd->bsd', h, W2[i]) + b2[i]
            out = out + yi * weights[..., i:i + 1]
        return out
    x = L0_attn_x
    x = x + 0.5 * _L0_ffn_ref(_layernorm(x, axis=-1), L0_ffn_Wr, L0_ffn_br, L0_ffn_W1, L0_ffn_b1, L0_ffn_W2, L0_ffn_b2)
    x = x + _L0_attn_ref(_layernorm(x, axis=-1), L0_attn_Wq, L0_attn_bq, L0_attn_Wk, L0_attn_bk, L0_attn_Wv, L0_attn_bv, L0_attn_Wo, L0_attn_bo)
    x = x + 0.5 * _L0_ffn_ref(_layernorm(x, axis=-1), L0_ffn_Wr, L0_ffn_br, L0_ffn_W1, L0_ffn_b1, L0_ffn_W2, L0_ffn_b2)
    return x

_drawn_inputs = setup_inputs


def setup_inputs(seed=0):
    import zlib

    import numpy as np

    out = dict(_drawn_inputs(seed))
    spreads = {}
    factors = {'L0_attn_Wq': 2.751, 'L0_attn_bq': 8.0, 'L0_attn_Wk': 2.67, 'L0_attn_bk': 8.0}
    for name, (base, spread) in spreads.items():
        noise = np.random.default_rng([zlib.crc32(name.encode()), seed]).standard_normal(out[name].shape)
        drawn = base * np.exp(spread * noise) if base else spread * noise
        out[name] = jnp.asarray(drawn.astype(out[name].dtype))
    for name, factor in factors.items():
        out[name] = (out[name] * factor).astype(out[name].dtype)
    return out
```

```python
from contextlib import ExitStack

import concourse.bass as bass
from concourse import mybir

F32 = mybir.dt.float32
BF16 = mybir.dt.bfloat16
I32 = mybir.dt.int32
ALU = mybir.AluOpType
ACT = mybir.ActivationFunctionType
AX = mybir.AxisListType

P = 128
F32R = mybir.dt.float32r
BANK = 512
TOKENS = 8 * 512
TT = TOKENS // P
NB = 8
S = 512
BT = S // P
HEADS = 16
HD = 8
G = 4
J = HEADS // G
D = 128
E = 8
H = 512
HC = H // P
TOPK = 2
SLOTS = 256
SB = SLOTS // P
NT = TOPK * TOKENS // SLOTS + E - 1
MAXT = TOKENS // SLOTS
EPS = 1e-5
W1_AT, W2_AT, B1_AT, B2_AT = 0, H, H + HC * D, H + HC * D + HC
WROW = B2_AT + D
RING = 8
ZROWS = 13


PARTS = 4 * HD
SHIFT = PARTS
DEN = HD

SPARE = {(0, 0): "turn_max", (0, 1): "spread_den", (0, 2): "turn_x", (0, 3): "q",
         (1, 0): "k", (1, 1): "turn_max", (1, 2): "project", (1, 3): "spread_den",
         (2, 0): "turn_max", (2, 1): "spread_den", (2, 2): "v",
         (3, 0): "turn_max", (3, 1): "spread_den"}


def build(nc, x_in, wr_in, br_in, experts, wqkv_in, wo_in, bqk_in, bvo_in, out):
    with ExitStack() as ctx:
        def sb(name, shape, dt=F32):
            return ctx.enter_context(nc.sbuf_tensor(name, shape, dt))

        def sem(name):
            return ctx.enter_context(nc.semaphore(name))

        psum = ctx.enter_context(nc.psum_tensor("psum", [P, 8, BANK], F32))
        slots_x = nc.dram_tensor("slots_x", [NT * SLOTS, D], F32).ap()
        slots_y = nc.dram_tensor("slots_y", [NT * SLOTS, D], F32).ap()

        x = sb("x", [P, TT, D])
        xn = sb("xn", [P, TT, D])
        stats = sb("stats", [P, TT, 6])
        meanvar = sb("meanvar", [P, TT, 2])
        var_eps = sb("var_eps", [P, TT])
        rstd = sb("rstd", [P, TT])
        neg_half = sb("neg_half", [P, TT])
        ident = sb("ident", [P, P])
        wr = sb("wr", [D, E])
        br = sb("br", [P, E])
        xnT = sb("xnT", [P, 2, BANK])
        before = sb("before", [P, P], BF16)
        ones_bf = sb("ones_bf", [P, P], BF16)
        e_rev = sb("e_rev", [P, TT, E])
        tile_steps = sb("tile_steps", [P, E, MAXT])
        tile_no = sb("tile_no", [P, NT, E])
        restart = sb("restart", [P, E, TT])
        ones_e = sb("ones_e", [P, E])
        score = sb("score", [P, TT, E])
        score2 = sb("score2", [P, TT, E])
        hit = sb("hit", [P, TT, E])
        pick = [sb(f"pick{j}", [P, TT, E]) for j in range(TOPK)]
        picked = sb("picked", [P, TT, E], BF16)
        best = [sb(f"best{j}", [P, TT]) for j in range(TOPK)]
        key = sb("key", [P, TT])
        gap = sb("gap", [P, TT])
        den = sb("den", [P, TT])
        weight = sb("weight", [P, TOPK, TT])
        totals = sb("totals", [P, E, TT])
        running = sb("running", [P, E, TT])
        fill = sb("fill", [P, E, MAXT])
        tiles_e = sb("tiles_e", [P, E])
        ends = sb("ends", [P, E])
        base = sb("base", [P, E])
        where = sb("where", [P, TT, E])
        where_j = sb("where_j", [P, TT, E])
        slot_f = sb("slot_f", [P, TOPK, TT])
        slot = sb("slot", [P, TOPK, TT], I32)
        past = sb("past", [P, NT, E])
        expert_f = sb("expert_f", [P, NT])
        expert = sb("expert", [P, NT], I32)
        w = sb("w", [P, 2, WROW])
        xs = sb("xs", [P, 2, SB, D])
        xsT = sb("xsT", [P, 2, SLOTS])
        hT = sb("hT", [P, 2, HC, SLOTS])
        ys = sb("ys", [P, 2, SB, D])
        rows = sb("rows", [P, RING, TOPK, D])

        qk_rows = nc.dram_tensor("qk_rows", [2, 2, P, S], F32).ap()
        max_rows = nc.dram_tensor("max_rows", [2, J, S], F32).ap()
        qx = sb("qx", [P, G, J, S], F32R)
        kx = sb("kx", [P, G, J, S], F32R)
        probs = xn[:].rearrange("p t d -> p (t d)").rearrange("p (b j s) -> p b j s", b=2, j=J)
        vx = sb("vx", [P, BT, HEADS, 32])
        v_rows = sb("v_rows", [P, BT, HEADS, HD])
        xb = sb("xb", [P, BT, D])
        xbT = sb("xbT", [P, S])
        q_parts = sb("q_parts", [P, 2, S], F32R)
        k_parts = sb("k_parts", [P, 2, S], F32R)
        zeros = sb("zeros", [2, J * S])
        neg_max = sb("neg_max", [P, 2, J, BT])
        max_parts = sb("max_parts", [J, 2, S], F32R)
        acc_sb = sb("acc_sb", [P, 2, S])
        recip = sb("recip", [P, S])
        attn = sb("attn", [P, G, S])
        wqkv = sb("wqkv", [D, 3, D])
        wo = sb("wo", [P, G, D])
        bqk = sb("bqk", [P, 2])
        bvo = sb("bvo", [P, 2, D])
        spread = sb("spread", [P, P])

        consts = sem("consts")
        sp_waited = sem("sp_waited")
        pool_waited = sem("pool_waited")
        at_consts = sem("at_consts")
        at_loaded = sem("at_loaded")
        wo_zero = sem("wo_zero")
        xb_ready = sem("xb_ready")
        xbT_ps = sem("xbT_ps")
        xbT_sb = sem("xbT_sb")
        qk_ps = sem("qk_ps")
        qk_high = sem("qk_high")
        qk_low = sem("qk_low")
        v_ps = sem("v_ps")
        v_sb = sem("v_sb")
        vx_ready = sem("vx_ready")
        bo_added = sem("bo_added")
        qk_stored = [sem(f"{n}_stored") for n in "qk"]
        qkx_in = [sem(f"qkx_in{g}") for g in range(G)]
        max_stored = sem("max_stored")
        max_in = [sem(f"max_in{g}") for g in range(G)]
        s_ps = sem("s_ps")
        s_max = sem("s_max")
        maxT_ps = sem("maxT_ps")
        max_sb = sem("max_sb")
        st_ps = sem("st_ps")
        exp_sb = sem("exp_sb")
        pv_ps = sem("pv_ps")
        acc_out = sem("acc_out")
        den_ps = sem("den_ps")
        recip_sb = sem("recip_sb")
        attn_sb = sem("attn_sb")
        o_ps = sem("o_ps")
        o_sb = sem("o_sb")
        max_high = sem("max_high")
        x_loaded = sem("x_loaded")
        rows_zero = sem("rows_zero")
        zeroed = sem("zeroed")
        dve_step = sem("dve_step")
        pool_step = sem("pool_step")
        var_ready = sem("var_ready")
        rstd_ready = sem("rstd_ready")
        xn_ready = sem("xn_ready")
        xnT_ps = sem("xnT_ps")
        xnT_sb = sem("xnT_sb")
        routed_ps = sem("routed_ps")
        gap_ready = sem("gap_ready")
        gap_exp = sem("gap_exp")
        picked_ready = sem("picked_ready")
        counts_ps = sem("counts_ps")
        slots_ready = sem("slots_ready")
        scattered = sem("scattered")
        w_in = [sem(f"w_in{i}") for i in range(2)]
        xs_in = [sem(f"xs_in{i}") for i in range(2)]
        xsT_ps = sem("xsT_ps")
        xsT_sb = sem("xsT_sb")
        h_ps = sem("h_ps")
        h_act = sem("h_act")
        h_dve = sem("h_dve")
        y_ps = sem("y_ps")
        y_sb = sem("y_sb")
        y_out = [sem(f"y_out{i}") for i in range(2)]
        gathered = [sem(f"gathered{i}") for i in range(RING)]
        combined = sem("combined")
        stored = sem("stored")

        ps_st = [psum[:, 2 * i:2 * i + 2, :] for i in range(2)]
        ps_s = [psum[:, 4 + i, :] for i in range(2)]
        ps_acc = psum[:, 6, :]
        ps_spare = psum[:, 7, :]
        ps_t = psum[:, 7, :]
        ps_h = [psum[:, 2 * i:2 * i + 2, :].rearrange("p a (b n) -> p (a b) n", b=2) for i in range(2)]
        ps_y = [psum[:, 4 + i, 0:SB * D].rearrange("p (s d) -> p s d", s=SB) for i in range(2)]
        ps_score = psum[:, 6, 0:TT * E].rearrange("p (t e) -> p t e", e=E)
        ps_rank = psum[:, 0, 0:TT * E].rearrange("p (t e) -> p t e", e=E)
        ps_total = psum[:, 1, 0:TT * E].rearrange("p (t e) -> p t e", e=E)

        slots_x_v = slots_x.rearrange("(n s p) d -> n p s d", p=P, s=SB)
        slots_y_v = slots_y.rearrange("(n s p) d -> n p s d", p=P, s=SB)
        x_v = x_in.rearrange("(t p) d -> p t d", p=P)
        out_v = out.rearrange("(t p) d -> p t d", p=P)
        PHASES = 2
        QKX = 16 * 5

        def one(i):
            return bass.ds(i, 1)

        def wait(eng, semaphore, count):
            if not isinstance(count, int) or count > 0:
                eng.wait_ge(semaphore, count)

        def wait_alone(eng, semaphore, count, carrier=sp_waited):
            if not isinstance(count, int) or count > 0:
                eng.wait_ge(semaphore, count)
                eng.sem_inc(carrier, 1)

        def sequences(eng, run):
            run(0, True, False)
            with eng.Fori(1, NB - 1) as b:
                run(b, False, False)
            run(NB - 1, False, True)

        def tasks(g, c, first, last):
            what = SPARE.get((g, c))
            if last and (what in ("turn_x", "q", "k", "v") or (what == "turn_max" and g == G - 1)):
                return None
            if first and (what == "project" or (what == "spread_den" and g == 0)):
                return None
            return what

        def done(n):
            return n + 3

        def laps(p, k):
            return (p * NT + 1 - k) // 2

        def tile_of(p, i, k):
            first = p * NT + k
            return 2 * i + first, first % 2, i + first // 2 + 1

        block = ctx.enter_context(nc.Block())

        @block.gpsimd
        def _(pool):
            n = [0]

            def step(ins):
                ins.then_inc(pool_step, 1)
                n[0] += 1
                pool.wait_ge(pool_step, n[0])

            step(nc.gpsimd.memset(ident[:], 0.0))
            step(nc.gpsimd.memset(before[:], 1.0))
            step(nc.gpsimd.affine_select(out=ident[:], in_=ident[:], compare_op=ALU.not_equal, fill=1.0,
                                         base=0, pattern=[[-1, P]], channel_multiplier=1))
            step(nc.gpsimd.affine_select(out=before[:], in_=before[:], compare_op=ALU.is_gt, fill=0.0,
                                         base=0, pattern=[[1, P]], channel_multiplier=-1))
            step(nc.gpsimd.memset(ones_bf[:], 1.0))
            step(nc.gpsimd.memset(neg_half[:], -0.5))
            step(nc.gpsimd.memset(ones_e[:], 1.0))
            step(nc.gpsimd.memset(restart[:], 1.0))
            step(nc.gpsimd.memset(restart[:, :, 0:1], 0.0))
            step(nc.gpsimd.iota(e_rev[:], [[0, TT], [-1, E]], base=E, channel_multiplier=0,
                                allow_small_or_imprecise_dtypes=True))
            step(nc.gpsimd.iota(tile_steps[:], [[0, E], [SLOTS, MAXT]], base=0, channel_multiplier=0,
                                allow_small_or_imprecise_dtypes=True))
            nc.gpsimd.iota(tile_no[:], [[1, NT], [0, E]], base=0, channel_multiplier=0,
                           allow_small_or_imprecise_dtypes=True).then_inc(consts, 1)
            step(nc.gpsimd.memset(spread[:], 0.0))
            step(nc.gpsimd.affine_select(out=spread[:].rearrange("p (j r) -> p j r", j=J), in_=spread[:].rearrange("p (j r) -> p j r", j=J),
                                         compare_op=ALU.not_equal, fill=1.0, base=-DEN, pattern=[[-32, J], [0, 32]],
                                         channel_multiplier=1))
            step(nc.gpsimd.memset(vx[:], 0.0))
            step(nc.gpsimd.memset(vx[:, :, :, DEN:DEN + 1], 1.0))
            step(nc.gpsimd.memset(qx[:].bitcast(F32), 0.0))
            step(nc.gpsimd.memset(kx[:].bitcast(F32), 0.0))
            step(nc.gpsimd.memset(kx[SHIFT:SHIFT + 2].bitcast(F32), 1.0))
            nc.gpsimd.memset(zeros[:], 0.0).then_inc(at_consts, 1)

            def expand_v(b, g):
                wait_alone(pool, pv_ps, 16 * b - 16 + 4 * g + 4, pool_waited)
                wait_alone(pool, v_sb, b + 1, pool_waited)
                nc.gpsimd.tensor_copy(vx[:, :, J * g:J * g + J, 0:HD], v_rows[:, :, J * g:J * g + J, :]).then_inc(vx_ready, 1)

            def normalize(b, g):
                u = 4 * b + g
                pool.wait_ge(recip_sb, u + 1)
                wait(pool, o_ps, b)
                nc.gpsimd.tensor_tensor(attn[:, g, :], acc_sb[:, g % 2, :], recip[:], ALU.mult).then_inc(attn_sb, 1)

            def add_bo(b):
                pool.wait_ge(xb_ready, b + 1)
                nc.gpsimd.tensor_tensor(x[:, bass.ds(4 * b, BT), :], x[:, bass.ds(4 * b, BT), :],
                                        bvo[:, 1:2, :].to_broadcast([P, BT, D]), ALU.add).then_inc(bo_added, 1)

            def attention():
                add_bo(0)
                for g in range(G):
                    expand_v(0, g)

                def run(b, first, last):
                    if not first:
                        normalize(b - 1, G - 1)
                        expand_v(b, G - 1)
                    if not last:
                        add_bo(b + 1)
                    for g in range(1, G):
                        normalize(b, g - 1)
                    if not last:
                        for g in range(G - 1):
                            expand_v(b + 1, g)

                sequences(pool, run)
                normalize(NB - 1, G - 1)

            for p in range(PHASES):
                if p == 1:
                    pool.wait_ge(var_ready, 2)
                    nc.gpsimd.tensor_tensor(rstd[:], var_eps[:], neg_half[:], ALU.pow).then_inc(rstd_ready, 1)
                    pool.wait_ge(at_loaded, 16 * (3 + J))
                    attention()
                pool.wait_ge(var_ready, 2 * p + 1)
                nc.gpsimd.tensor_tensor(rstd[:], var_eps[:], neg_half[:], ALU.pow).then_inc(rstd_ready, 1)
                if p == 0:
                    pool.wait_ge(zeroed, 16 * (NT * SB // ZROWS))
                pool.wait_ge(slots_ready, p + 1)
                for t in range(TT):
                    for j in range(TOPK):
                        nc.gpsimd.indirect_dma_start(
                            slots_x, bass.IndirectOffsetOnAxis(ap=slot[:, j, t:t + 1], axis=0),
                            xn[:, t, :], None).then_inc(scattered, 16)
                for k in range(2):
                    pool.wait_ge(y_out[k], 16 * (laps(p + 1, k) + 1))
                for t in range(TT):
                    g = p * TT + t
                    if g >= RING:
                        pool.wait_ge(combined, g - RING + 1)
                    for j in range(TOPK):
                        nc.gpsimd.indirect_dma_start(
                            rows[:, g % RING, j, :], None, slots_y,
                            bass.IndirectOffsetOnAxis(ap=slot[:, j, t:t + 1], axis=0)).then_inc(gathered[g % RING], 16)

        @block.sync
        def _(sp):
            sp.dma_start(x[:], x_v).then_inc(x_loaded, 16)
            sp.dma_start(wr[:], wr_in).then_inc(x_loaded, 16)
            sp.dma_start(br[:], br_in.partition_broadcast(P)).then_inc(x_loaded, 16)
            sp.wait_ge(rows_zero, 1)
            zero = rows[:].rearrange("p a b d -> p (a b d)")[:, 0:ZROWS * D]
            for z in range(NT * SB // ZROWS):
                sp.dma_start(slots_x[z * ZROWS * P:(z + 1) * ZROWS * P].rearrange("(p r) d -> p (r d)", p=P),
                             zero).then_inc(zeroed, 16)

            sp.dma_start(wqkv[:], wqkv_in).then_inc(at_loaded, 16)
            sp.dma_start(bqk[:], bqk_in).then_inc(at_loaded, 16)
            sp.dma_start(bvo[:], bvo_in.partition_broadcast(P)).then_inc(at_loaded, 16)
            sp.wait_ge(wo_zero, 1)
            wo_v = wo_in.rearrange("(g j r) n -> j r g n", g=G, j=J)
            for j in range(J):
                sp.dma_start(wo[32 * j:32 * j + HD, :, :], wo_v[j]).then_inc(at_loaded, 16)

            def store_qk(b, which):
                wait_alone(sp, qk_low, 2 * b + which + 1)
                for g in range(G):
                    wait_alone(sp, qkx_in[g], QKX * b)
                parts = (q_parts, k_parts)[which]
                sp.dma_start(qk_rows[which].rearrange("h p n -> p h n"), parts[:].bitcast(F32)).then_inc(qk_stored[which], 16)

            def expand_qk(b, g):
                for s in qk_stored:
                    wait_alone(sp, s, 16 * (b + 1))
                wait_alone(sp, st_ps, 32 * b - 32 + 8 * g + 8)
                q_of, k_of = (qk_rows[i].rearrange("h (d g j) n -> g h d (j n)", d=HD, g=G)[g] for i in range(2))
                for h in range(2):
                    sp.dma_start(qx[2 * HD * h:2 * HD * (h + 1), g, :, :].rearrange("p j n -> p (j n)").bitcast(F32),
                                 q_of[h].unsqueeze(0).to_broadcast([2, HD, J * S])).then_inc(qkx_in[g], 16)
                for r in range(2):
                    sp.dma_start(kx[2 * HD * r:2 * HD * (r + 1), g, :, :].rearrange("p j n -> p (j n)").bitcast(F32), k_of).then_inc(qkx_in[g], 16)
                sp.dma_start(qx[SHIFT:SHIFT + 2, g, :, :].rearrange("p j n -> p (j n)").bitcast(F32), zeros[:]).then_inc(qkx_in[g], 16)

            def place_max(b, g):
                u = 4 * b + g
                wait_alone(sp, max_sb, u + 1)
                if g:
                    wait_alone(sp, max_in[g - 1], 16 * (b + 1))
                else:
                    wait_alone(sp, max_in[G - 1], 16 * b)
                sp.dma_start(max_rows.rearrange("h j n -> j h n"), max_parts[:].bitcast(F32)).then_inc(max_stored, 16)
                wait_alone(sp, max_stored, 16 * (u + 1))
                sp.dma_start(qx[SHIFT:SHIFT + 2, g, :, :].rearrange("p j n -> p (j n)").bitcast(F32),
                             max_rows.rearrange("h j n -> h (j n)")).then_inc(max_in[g], 16)

            def attention():
                store_qk(0, 0)
                store_qk(0, 1)
                for g in range(G - 1):
                    expand_qk(0, g)
                place_max(0, 0)

                def run(b, first, last):
                    expand_qk(b, G - 1)
                    place_max(b, 1)
                    if not last:
                        store_qk(b + 1, 0)
                        store_qk(b + 1, 1)
                        expand_qk(b + 1, 0)
                    place_max(b, 2)
                    if not last:
                        expand_qk(b + 1, 1)
                    place_max(b, 3)
                    if not last:
                        expand_qk(b + 1, 2)
                        place_max(b + 1, 0)

                sequences(sp, run)

            def load(p, i, k):
                n, b, _ = tile_of(p, i, k)
                e = sp.value_load(expert[0:1, one(2 * i + k)], min_val=0, max_val=E - 1)
                wait_alone(sp, xsT_ps, done(n - 2))
                sp.dma_start(xs[:, b, :, :], slots_x_v[one(2 * i + k)].rearrange("n p s d -> p (n s) d")).then_inc(xs_in[b], 16)
                wait_alone(sp, y_sb, done(n - 2))
                sp.dma_start(w[:, b, :], experts[one(e)].rearrange("e p n -> p (e n)")).then_inc(w_in[b], 16)

            for p in range(PHASES):
                if p == 1:
                    sp.wait_ge(at_consts, 1)
                    attention()
                sp.wait_ge(slots_ready, p + 1)
                sp.wait_ge(scattered, 16 * TOPK * TT * (p + 1))
                with sp.Fori(0, NT // 2) as i:
                    load(p, i, 0)
                    load(p, i, 1)
                load(p, NT // 2, 0)
            for q in range(TT // 4):
                sp.wait_ge(combined, TT + 4 * q + 4)
                sp.dma_start(out_v[:, 4 * q:4 * q + 4, :], x[:, 4 * q:4 * q + 4, :]).then_inc(stored, 16)
            sp.wait_ge(stored, 16 * (TT // 4))

        @block.scalar
        def _(act):
            def front(p):
                with act.Fori(0, TT // 8) as i:
                    for k in range(2):
                        g = p * (TT // 4) + 2 * i + k
                        act.wait_ge(xnT_ps, g + 1)
                        act.wait_ge(routed_ps, done(g - 2))
                        nc.scalar.activation(xnT[:, k, :], ps_t, ACT.Copy).then_inc(xnT_sb, 1)
                act.wait_ge(gap_ready, p + 1)
                nc.scalar.activation(gap[:], gap[:], ACT.Exp).then_inc(gap_exp, 1)

            def hidden(p, i, k):
                n, b, _ = tile_of(p, i, k)
                act.wait_ge(xsT_ps, done(n))
                act.wait_ge(h_ps, done(n - 2))
                nc.scalar.activation(xsT[:, b, :], ps_t[:, 0:SLOTS], ACT.Copy).then_inc(xsT_sb, 1)
                act.wait_ge(h_ps, done(n))
                act.wait_ge(y_ps, done(n - 2))
                for c in range(HC // 2):
                    last = nc.scalar.activation(hT[:, b, c, :], ps_h[b][:, c, :], ACT.Relu,
                                                bias=w[:, b, B1_AT + c:B1_AT + c + 1])
                last.then_inc(h_act, 1)

            def store(p, i, k):
                n, b, _ = tile_of(p, i, k)
                act.wait_ge(y_sb, done(n))
                act.dma_start(slots_y_v[one(2 * i + k)].rearrange("n p s d -> p (n s) d"), ys[:, b, :, :]).then_inc(y_out[b], 16)

            def turn_x_out(b):
                act.wait_ge(xbT_ps, b + 1)
                wait(act, v_ps, b)
                nc.scalar.activation(xbT[:], ps_spare, ACT.Copy).then_inc(xbT_sb, 1)

            def high(b, which):
                act.wait_ge(qk_ps, 2 * b + which + 1)
                wait(act, qk_stored[which], 16 * b)
                parts = (q_parts, k_parts)[which]
                nc.scalar.activation(parts[:, 0, :], ps_spare, ACT.Identity, bias=bqk[:, which:which + 1]).then_inc(qk_high, 1)

            def exps(b, g, c, half):
                step = 16 * b + 4 * g + c
                act.wait_ge(st_ps, 2 * step + half + 1)
                wait(act, pv_ps, step - 1)
                nc.scalar.activation(probs[:, c % 2, 2 * half:2 * half + 2, :], ps_st[half], ACT.Exp,
                                     scale=HD ** -0.5).then_inc(exp_sb, 1)

            def acc_done(b, g):
                u = 4 * b + g
                act.wait_ge(pv_ps, 4 * u + 4)
                wait(act, attn_sb, u - 1)
                nc.scalar.activation(acc_sb[:, g % 2, :], ps_acc, ACT.Copy).then_inc(acc_out, 1)

            def attention():
                turn_x_out(0)
                high(0, 0)
                high(0, 1)

                def run(b, first, last):
                    for g in range(G):
                        for c in range(BT):
                            exps(b, g, c, 0)
                            what = tasks(g, c - 1, first, last) if c else tasks(g - 1, BT - 1, first, last)
                            if what == "turn_x":
                                turn_x_out(b + 1)
                            elif what == "q":
                                high(b + 1, 0)
                            elif what == "k":
                                high(b + 1, 1)
                            exps(b, g, c, 1)
                            if c == 0 and not (first and g == 0):
                                acc_done(b - (g == 0), (g - 1) % G)

                sequences(act, run)
                acc_done(NB - 1, G - 1)

            for s in (xnT_sb, xsT_sb, h_act):
                act.sem_inc(s, 2)
            for s in y_out:
                act.sem_inc(s, 16)
            for p in range(PHASES):
                if p == 1:
                    attention()
                front(p)
                hidden(p, 0, 0)
                with act.Fori(0, NT // 2) as i:
                    hidden(p, i, 1)
                    store(p, i, 0)
                    hidden(p, i, 2)
                    store(p, i, 1)
                store(p, NT // 2, 0)

        @block.tensor
        def _(pe):
            for s in (routed_ps, xsT_ps, h_ps, y_ps):
                pe.sem_inc(s, 2)

            def front(p):
                for q in range(TT // 4):
                    g = p * (TT // 4) + q
                    pe.wait_ge(xn_ready, g + 1)
                    pe.wait_ge(xnT_sb, done(g - 1))
                    for j in range(4):
                        mm = nc.tensor.transpose(ps_t[:, j * P:(j + 1) * P], xn[:, 4 * q + j, :], ident[:])
                    mm.then_inc(xnT_ps, 1)
                    pe.wait_ge(xnT_sb, done(g))
                    for j in range(4):
                        mm = nc.tensor.matmul(ps_score[:, 4 * q + j, :], xnT[:, q % 2, j * P:(j + 1) * P], wr[:],
                                              start=True, stop=True)
                    mm.then_inc(routed_ps, 1)
                pe.wait_ge(picked_ready, p + 1)
                rhs = picked[:].rearrange("p t e -> p (t e)")
                nc.tensor.matmul(psum[:, 0, 0:TT * E], before[:], rhs, start=True, stop=True)
                nc.tensor.matmul(psum[:, 1, 0:TT * E], ones_bf[:], rhs, start=True, stop=True).then_inc(counts_ps, 1)

            def up(p, i, k):
                n, b, lap = tile_of(p, i, k)
                pe.wait_ge(xs_in[b], 16 * lap)
                pe.wait_ge(xsT_sb, done(n - 1))
                for s in range(SB):
                    mm = nc.tensor.transpose(ps_t[:, s * P:(s + 1) * P], xs[:, b, s, :], ident[:])
                mm.then_inc(xsT_ps, 1)
                pe.wait_ge(xsT_sb, done(n))
                pe.wait_ge(w_in[b], 16 * lap)
                pe.wait_ge(h_act, done(n - 2))
                pe.wait_ge(h_dve, done(n - 2))
                for c in range(HC):
                    mm = nc.tensor.matmul(ps_h[b][:, c, :], w[:, b, W1_AT + c * P:W1_AT + (c + 1) * P], xsT[:, b, :],
                                          start=True, stop=True)
                mm.then_inc(h_ps, 1)

            def down(p, i, k):
                n, b, _ = tile_of(p, i, k)
                pe.wait_ge(h_act, done(n))
                pe.wait_ge(h_dve, done(n))
                pe.wait_ge(y_sb, done(n - 2))
                for s in range(SB):
                    for c in range(HC):
                        mm = nc.tensor.matmul(ps_y[b][:, s, :], hT[:, b, c, s * P:(s + 1) * P],
                                              w[:, b, W2_AT + c * D:W2_AT + (c + 1) * D], start=(c == 0), stop=(c == HC - 1))
                mm.then_inc(y_ps, 1)

            def turn_x(b):
                pe.wait_ge(xb_ready, b + 1)
                for j in range(BT):
                    mm = nc.tensor.transpose(ps_spare[:, j * P:(j + 1) * P], xb[:, j, :], ident[:])
                mm.then_inc(xbT_ps, 1)

            def project_qk(b, which):
                pe.wait_ge(xbT_sb, b + 1)
                nc.tensor.matmul(ps_spare, wqkv[:, which, :], xbT[:], start=True, stop=True).then_inc(qk_ps, 1)

            def project_v(b):
                for j in range(BT):
                    mm = nc.tensor.matmul(ps_spare[:, j * P:(j + 1) * P], xbT[:, j * P:(j + 1) * P], wqkv[:, 2, :],
                                          start=True, stop=True)
                mm.then_inc(v_ps, 1)

            def project_out(b):
                pe.wait_ge(attn_sb, 4 * b + 4)
                for j in range(BT):
                    for g in range(G):
                        mm = nc.tensor.matmul(ps_spare[:, j * P:(j + 1) * P], attn[:, g, j * P:(j + 1) * P], wo[:, g, :],
                                              start=(g == 0), stop=(g == G - 1))
                mm.then_inc(o_ps, 1)

            def turn_max(b, g):
                pe.wait_ge(s_max, 16 * (4 * b + g) + 16)
                for c in range(BT):
                    mm = nc.tensor.transpose(ps_spare[0:J, c * P:(c + 1) * P], neg_max[:, g % 2, :, c], ident[:])
                mm.then_inc(maxT_ps, 1)

            def spread_den(b, g):
                pe.wait_ge(acc_out, 4 * b + g + 1)
                nc.tensor.matmul(ps_spare, spread[:], acc_sb[:, g % 2, :], start=True, stop=True).then_inc(den_ps, 1)

            def scores(b, g, j, c):
                if j == 0 and c == 0:
                    pe.wait_ge(qkx_in[g], QKX * (b + 1))
                block = 16 * (4 * b + g) + 4 * j + c
                wait(pe, s_max, block - 1)
                nc.tensor.matmul(ps_s[c % 2], qx[:, g, j, c * P:(c + 1) * P], kx[:, g, j, :],
                                 start=True, stop=True).then_inc(s_ps, 1)

            def shifted(b, g, c, half):
                if c == 0 and half == 0:
                    pe.wait_ge(max_in[g], 16 * (b + 1))
                wait(pe, exp_sb, 2 * (16 * b + 4 * g + c) + half - 1)
                for i in range(2):
                    j = 2 * half + i
                    mm = nc.tensor.matmul(ps_st[half][:, i, :], kx[:, g, j, c * P:(c + 1) * P], qx[:, g, j, :],
                                          start=True, stop=True)
                mm.then_inc(st_ps, 1)

            def values(b, g, c):
                u = 4 * b + g
                pe.wait_ge(exp_sb, 2 * (4 * u + c) + 2)
                if c == 0:
                    pe.wait_ge(vx_ready, u + 1)
                    wait(pe, acc_out, u)
                for j in range(J):
                    mm = nc.tensor.matmul(ps_acc[32 * j:32 * j + 32, :], vx[:, c, J * g + j, :], probs[:, c % 2, j, :],
                                          start=(c == 0), stop=(c == BT - 1))
                mm.then_inc(pv_ps, 1)

            def attention():
                pe.wait_ge(at_loaded, 16 * (3 + J))
                pe.wait_ge(at_consts, 1)
                turn_x(0)
                project_qk(0, 0)
                pe.wait_ge(qk_low, 1)
                project_qk(0, 1)
                pe.wait_ge(qk_low, 2)
                project_v(0)
                for u in range(2):
                    for j in range(J):
                        for c in range(BT):
                            scores(0, u, j, c)
                pe.wait_ge(v_sb, 1)
                turn_max(0, 0)

                def run(b, first, last):
                    for g in range(G):
                        ahead = not (last and g >= 2)
                        for c in range(BT):
                            for half in range(2):
                                shifted(b, g, c, half)
                                if ahead:
                                    for i in range(2):
                                        scores(b + (g + 2) // G, (g + 2) % G, c, 2 * half + i)
                            if c:
                                values(b, g, c - 1)
                            elif not (first and g == 0):
                                values(b - (g == 0), (g - 1) % G, BT - 1)
                            spare_task(b, g, c, first, last)

                sequences(pe, run)
                values(NB - 1, G - 1, BT - 1)
                pe.wait_ge(recip_sb, 4 * NB - 1)
                spread_den(NB - 1, G - 1)
                pe.wait_ge(recip_sb, 4 * NB)
                project_out(NB - 1)

            def spare_task(b, g, c, first, last):
                what = tasks(g, c, first, last)
                before = None
                at = 4 * g + c - 1
                while what and before is None and at >= 0:
                    before = tasks(at // 4, at % 4, first, last)
                    at -= 1
                if before is None and what:
                    wait(pe, recip_sb, 4 * b - 1)
                    if first:
                        pe.wait_ge(max_sb, 1)
                    bg = 0
                elif what:
                    bg = (at + 1) // 4
                if before == "turn_max":
                    pe.wait_ge(max_sb, 4 * b + bg + 2)
                elif before == "spread_den":
                    pe.wait_ge(recip_sb, 4 * b + bg)
                elif before == "turn_x":
                    pe.wait_ge(xbT_sb, b + 2)
                elif before == "q":
                    pe.wait_ge(qk_low, 2 * b + 3)
                elif before == "k":
                    pe.wait_ge(qk_low, 2 * b + 4)
                elif before == "project":
                    pe.wait_ge(o_sb, b)
                elif before == "v":
                    pe.wait_ge(v_sb, b + 2)
                if what == "turn_max":
                    turn_max(b + (g + 1) // G, (g + 1) % G)
                elif what == "spread_den":
                    spread_den(b - (g == 0), (g - 1) % G)
                elif what == "turn_x":
                    turn_x(b + 1)
                elif what == "q":
                    project_qk(b + 1, 0)
                elif what == "k":
                    project_qk(b + 1, 1)
                elif what == "v":
                    project_v(b + 1)
                elif what == "project":
                    project_out(b - 1)

            pe.wait_ge(consts, 1)
            pe.wait_ge(x_loaded, 48)
            for p in range(PHASES):
                if p == 1:
                    attention()
                front(p)
                up(p, 0, 0)
                with pe.Fori(0, NT // 2) as i:
                    up(p, i, 1)
                    down(p, i, 0)
                    up(p, i, 2)
                    down(p, i, 1)
                down(p, NT // 2, 0)

        @block.vector
        def _(dve):
            n = [0]

            def step(ins):
                ins.then_inc(dve_step, 1)
                n[0] += 1
                dve.wait_ge(dve_step, n[0])

            nc.vector.memset(rows[:], 0.0).then_inc(rows_zero, 1)
            nc.vector.memset(wo[:], 0.0).then_inc(wo_zero, 1)
            for s in (h_dve, y_sb):
                dve.sem_inc(s, 2)
            dve.wait_ge(x_loaded, 48)
            dve.wait_ge(consts, 1)

            def statistics(k):
                for t in range(TT):
                    last = nc.vector.bn_stats(stats[:, t, :], x[:, t, :])
                step(last)
                for t in range(TT):
                    last = nc.vector.bn_aggr(meanvar[:, t, :], stats[:, t, :])
                step(last)
                nc.vector.tensor_scalar(var_eps[:], meanvar[:, :, 1], EPS, None, ALU.add).then_inc(var_ready, 1)
                dve.wait_ge(rstd_ready, k + 1)

            def front(p):
                statistics(2 * p)
                with dve.Fori(0, TT // 4) as i:
                    for j in range(4):
                        last = nc.vector.tensor_scalar(
                            xn[:, one(4 * i + j), :], x[:, one(4 * i + j), :],
                            meanvar[:, one(4 * i + j), 0], rstd[:, one(4 * i + j)], ALU.subtract, ALU.mult)
                    last.then_inc(xn_ready, 1)

            def route(p):
                def over_e(ap):
                    return ap.unsqueeze(2).to_broadcast([P, TT, E])

                dve.wait_ge(routed_ps, done((p + 1) * (TT // 4) - 1))
                step(nc.vector.tensor_tensor(score[:], ps_score, br[:].unsqueeze(1).to_broadcast([P, TT, E]), ALU.add))
                for j in range(TOPK):
                    s = score if j == 0 else score2
                    step(nc.vector.tensor_reduce(best[j][:], s[:], AX.X, ALU.max))
                    step(nc.vector.tensor_tensor(hit[:], s[:], over_e(best[j][:]), ALU.is_equal))
                    step(nc.vector.tensor_tensor(hit[:], hit[:], e_rev[:], ALU.mult))
                    step(nc.vector.tensor_reduce(key[:], hit[:], AX.X, ALU.max))
                    step(nc.vector.tensor_tensor(pick[j][:], e_rev[:], over_e(key[:]), ALU.is_equal))
                    if j == 0:
                        step(nc.vector.scalar_tensor_tensor(score2[:], pick[0][:], -3e38, score[:], ALU.mult, ALU.add))
                nc.vector.tensor_tensor(picked[:], pick[0][:], pick[1][:], ALU.add).then_inc(picked_ready, 1)
                nc.vector.tensor_tensor(gap[:], best[1][:], best[0][:], ALU.subtract).then_inc(gap_ready, 1)
                dve.wait_ge(gap_exp, p + 1)
                step(nc.vector.tensor_scalar(den[:], gap[:], 1.0, None, ALU.add))
                step(nc.vector.reciprocal(den[:], den[:]))
                step(nc.vector.tensor_scalar(weight[:, 0, :], den[:], 0.5, None, ALU.mult))
                step(nc.vector.tensor_tensor(weight[:, 1, :], weight[:, 0, :], gap[:], ALU.mult))
                dve.wait_ge(counts_ps, p + 1)
                step(nc.vector.tensor_copy(totals[:], ps_total.rearrange("p t e -> p e t")))
                step(nc.vector.tensor_tensor_scan(running[:].rearrange("p e t -> p (e t)"), restart[:].rearrange("p e t -> p (e t)"),
                                                  totals[:].rearrange("p e t -> p (e t)"), 0.0, ALU.mult, ALU.add))
                step(nc.vector.tensor_tensor(fill[:], running[:, :, TT - 1:TT].to_broadcast([P, E, MAXT]), tile_steps[:], ALU.is_gt))
                step(nc.vector.tensor_reduce(tiles_e[:], fill[:], AX.X, ALU.add))
                step(nc.vector.tensor_tensor_scan(ends[:], ones_e[:], tiles_e[:], 0.0, ALU.mult, ALU.add))
                step(nc.vector.tensor_tensor(base[:], ends[:], tiles_e[:], ALU.subtract))
                step(nc.vector.tensor_scalar(base[:], base[:], float(SLOTS), None, ALU.mult))
                step(nc.vector.tensor_tensor(running[:], running[:], totals[:], ALU.subtract))
                step(nc.vector.tensor_tensor(running[:], running[:], base[:].unsqueeze(2).to_broadcast([P, E, TT]), ALU.add))
                step(nc.vector.tensor_tensor(where[:], ps_rank, running[:].rearrange("p e t -> p t e"), ALU.add))
                for j in range(TOPK):
                    step(nc.vector.tensor_tensor(where_j[:], where[:], pick[j][:], ALU.mult))
                    step(nc.vector.tensor_reduce(slot_f[:, j, :], where_j[:], AX.X, ALU.add))
                nc.vector.tensor_copy(slot[:], slot_f[:])
                step(nc.vector.tensor_tensor(past[:], tile_no[:], ends[:].unsqueeze(1).to_broadcast([P, NT, E]), ALU.is_ge))
                step(nc.vector.tensor_reduce(expert_f[:], past[:], AX.X, ALU.add))
                nc.vector.tensor_scalar(expert[:], expert_f[:], float(E - 1), None, ALU.min).then_inc(slots_ready, 1)

            def hidden(p, i, k):
                n, b, _ = tile_of(p, i, k)
                dve.wait_ge(h_ps, done(n))
                dve.wait_ge(y_ps, done(n - 2))
                for c in range(HC // 2, HC):
                    last = nc.vector.tensor_scalar(hT[:, b, c, :], ps_h[b][:, c, :], w[:, b, B1_AT + c:B1_AT + c + 1], 0.0,
                                                   ALU.add, ALU.max)
                last.then_inc(h_dve, 1)

            def result(p, i, k):
                n, b, lap = tile_of(p, i, k)
                dve.wait_ge(y_ps, done(n))
                dve.wait_ge(y_out[b], 16 * lap)
                nc.vector.tensor_tensor(ys[:, b, :, :], ps_y[b], w[:, b, B2_AT:B2_AT + D].unsqueeze(1).to_broadcast([P, SB, D]),
                                        ALU.add).then_inc(y_sb, 1)

            def combine(p):
                for t in range(TT):
                    g = p * TT + t
                    dve.wait_ge(gathered[g % RING], 32 * (g // RING + 1))
                    step(nc.vector.scalar_tensor_tensor(x[:, t, :], rows[:, g % RING, 0, :], weight[:, 0, t:t + 1], x[:, t, :],
                                                        ALU.mult, ALU.add))
                    nc.vector.scalar_tensor_tensor(x[:, t, :], rows[:, g % RING, 1, :], weight[:, 1, t:t + 1], x[:, t, :],
                                                   ALU.mult, ALU.add).then_inc(combined, 1)
                dve.wait_ge(combined, (p + 1) * TT)

            def norm_x(b):
                wait(dve, xbT_ps, b)
                for j in range(BT):
                    t = 4 * b + j
                    last = nc.vector.tensor_scalar(xb[:, j, :], x[:, one(t), :], meanvar[:, one(t), 0], rstd[:, one(t)],
                                                   ALU.subtract, ALU.mult)
                last.then_inc(xb_ready, 1)

            def low(b, which):
                dve.wait_ge(qk_high, 2 * b + which + 1)
                parts = (q_parts, k_parts)[which]
                nc.vector.scalar_tensor_tensor(parts[:, 1, :], ps_spare, bqk[:, which:which + 1], parts[:, 0, :].bitcast(F32),
                                               ALU.add, ALU.subtract).then_inc(qk_low, 1)

            def v_done(b):
                dve.wait_ge(v_ps, b + 1)
                wait(dve, vx_ready, 4 * b)
                nc.vector.tensor_tensor(v_rows[:].rearrange("p t h d -> p t (h d)"), ps_spare.rearrange("p (t n) -> p t n", t=BT),
                                        bvo[:, 0:1, :].to_broadcast([P, BT, D]), ALU.add).then_inc(v_sb, 1)

            def maximum(b, g, j, c):
                block = 16 * (4 * b + g) + 4 * j + c
                dve.wait_ge(s_ps, block + 1)
                if j == 0 and c == 0:
                    wait(dve, maxT_ps, 4 * b + g - 1)
                nc.vector.tensor_reduce(neg_max[:, g % 2, j, c:c + 1], ps_s[c % 2], AX.X, ALU.max, negate=True).then_inc(s_max, 1)

            def max_done(b, g):
                u = 4 * b + g
                dve.wait_ge(maxT_ps, u + 1)
                wait(dve, max_stored, 16 * u)
                step_counted(nc.vector.tensor_copy(max_parts[:, 0, :], ps_spare[0:J, :]), max_high, u + 1)
                nc.vector.tensor_tensor(max_parts[:, 1, :], ps_spare[0:J, :], max_parts[:, 0, :].bitcast(F32),
                                        ALU.subtract).then_inc(max_sb, 1)

            def step_counted(ins, semaphore, count):
                ins.then_inc(semaphore, 1)
                dve.wait_ge(semaphore, count)

            def den_done(b, g):
                u = 4 * b + g
                dve.wait_ge(den_ps, u + 1)
                wait(dve, attn_sb, u)
                nc.vector.reciprocal(recip[:], ps_spare).then_inc(recip_sb, 1)

            def out_done(b):
                dve.wait_ge(o_ps, b + 1)
                dve.wait_ge(bo_added, b + 1)
                xs4 = x[:, bass.ds(4 * b, BT), :]
                nc.vector.tensor_tensor(xs4, ps_spare.rearrange("p (t n) -> p t n", t=BT), xs4, ALU.add).then_inc(o_sb, 1)

            def attention():
                norm_x(0)
                low(0, 0)
                low(0, 1)
                v_done(0)
                for u in range(2):
                    for j in range(J):
                        for c in range(BT):
                            maximum(0, u, j, c)
                max_done(0, 0)

                def finish(b, g, what):
                    if what == "turn_max":
                        max_done(b + (g + 1) // G, (g + 1) % G)
                    elif what == "spread_den":
                        den_done(b - (g == 0), (g - 1) % G)
                    elif what == "q":
                        low(b + 1, 0)
                    elif what == "k":
                        low(b + 1, 1)
                    elif what == "v":
                        v_done(b + 1)
                    elif what == "project":
                        out_done(b - 1)

                def run(b, first, last):
                    for g in range(G):
                        ahead = not (last and g >= 2)
                        for c in range(BT):
                            for i in range(BT):
                                if ahead:
                                    maximum(b + (g + 2) // G, (g + 2) % G, c, i)
                                if i == 1:
                                    at = 4 * g + c - 1
                                    if at >= 0:
                                        finish(b, at // 4, tasks(at // 4, at % 4, first, last))
                                    if at == 0 and not last:
                                        norm_x(b + 1)

                sequences(dve, run)
                den_done(NB - 1, G - 1)
                out_done(NB - 1)
                dve.wait_ge(o_sb, NB)

            for p in range(PHASES):
                if p == 1:
                    statistics(1)
                    attention()
                front(p)
                route(p)
                hidden(p, 0, 0)
                with dve.Fori(0, NT // 2) as i:
                    hidden(p, i, 1)
                    result(p, i, 0)
                    hidden(p, i, 2)
                    result(p, i, 1)
                result(p, NT // 2, 0)
                combine(p)


def kernel(**inputs):
    import numpy as np
    import concourse.bacc as bacc
    from concourse.bass_utils import run_bass_kernel_spmd

    a = {k: np.asarray(v) for k, v in inputs.items()}
    w1, w2 = a["L0_ffn_W1"], a["L0_ffn_W2"]
    experts = np.concatenate([
        w1,
        w2.reshape(E, HC, P, D).transpose(0, 2, 1, 3).reshape(E, P, HC * D),
        a["L0_ffn_b1"].reshape(E, HC, P).transpose(0, 2, 1),
        np.broadcast_to(a["L0_ffn_b2"][:, None, :], (E, P, D)),
    ], axis=2)
    by_dim = np.arange(D).reshape(HEADS, HD).T.ravel()
    wqkv = np.stack([a["L0_attn_Wq"].T[:, by_dim], a["L0_attn_Wk"].T[:, by_dim], a["L0_attn_Wv"].T], axis=1)
    bqk = np.stack([a["L0_attn_bq"][by_dim], a["L0_attn_bk"][by_dim]], axis=1)
    bvo = np.stack([a["L0_attn_bv"], a["L0_attn_bo"]])
    attn = {"wqkv": wqkv, "wo": a["L0_attn_Wo"].T, "bqk": bqk, "bvo": bvo}
    arrays = {"x": a["L0_attn_x"].reshape(TOKENS, D), "wr": a["L0_ffn_Wr"], "br": a["L0_ffn_br"], "experts": experts, **attn}
    arrays = {k: np.ascontiguousarray(v) for k, v in arrays.items()}
    nc = bacc.Bacc("TRN2", target_bir_lowering=False, num_devices=1)
    t = {k: nc.dram_tensor("in_" + k, v.shape, F32, kind="ExternalInput").ap() for k, v in arrays.items()}
    out = nc.dram_tensor("out", (TOKENS, D), F32, kind="ExternalOutput").ap()
    build(nc, t["x"], t["wr"], t["br"], t["experts"], t["wqkv"], t["wo"], t["bqk"], t["bvo"], out)
    r = run_bass_kernel_spmd(nc, [{"in_" + k: v for k, v in arrays.items()}], core_ids=[0])
    return r.results[0]["out"].reshape(8, 512, D)
```

```python
from contextlib import ExitStack

import concourse.bass as bass
from concourse import mybir

F32 = mybir.dt.float32
BF16 = mybir.dt.bfloat16
I32 = mybir.dt.int32
ALU = mybir.AluOpType
ACT = mybir.ActivationFunctionType
AX = mybir.AxisListType

P = 128
F32R = mybir.dt.float32r
BANK = 512
TOKENS = 8 * 512
TT = TOKENS // P
NB = 8
S = 512
BT = S // P
HEADS = 16
HD = 8
G = 4
J = HEADS // G
D = 128
E = 8
H = 512
HC = H // P
TOPK = 2
SLOTS = 256
SB = SLOTS // P
NT = TOPK * TOKENS // SLOTS + E - 1
MAXT = TOKENS // SLOTS
EPS = 1e-5
UP = H + HC
B2_AT = HC * D
WROW = UP + B2_AT + D
BLOCKS = NT * SB
AHEAD = 4
RING = 8


PARTS = 4 * HD
SHIFT = PARTS
DEN = HD

SPARE = {(0, 0): "turn_max", (0, 1): "spread_den", (0, 2): "turn_x", (0, 3): "q",
         (1, 0): "k", (1, 1): "turn_max", (1, 2): "project", (1, 3): "spread_den",
         (2, 0): "turn_max", (2, 1): "spread_den", (2, 2): "v",
         (3, 0): "turn_max", (3, 1): "spread_den"}


def build(nc, x_in, wr_in, br_in, experts, wqkv_in, wo_in, bqk_in, bvo_in, out):
    with ExitStack() as ctx:
        def sb(name, shape, dt=F32):
            return ctx.enter_context(nc.sbuf_tensor(name, shape, dt))

        def sem(name):
            return ctx.enter_context(nc.semaphore(name))

        psum = ctx.enter_context(nc.psum_tensor("psum", [P, 8, BANK], F32))
        xn_rows = nc.dram_tensor("xn_rows", [TOKENS, D], F32).ap()
        slots_y = nc.dram_tensor("slots_y", [NT * SLOTS, D], F32).ap()

        x = sb("x", [P, TT, D])
        xn = sb("xn", [P, TT, D])
        stats = sb("stats", [P, TT, 6])
        meanvar = sb("meanvar", [P, TT, 2])
        var_eps = sb("var_eps", [P, TT])
        rstd = sb("rstd", [P, TT])
        weight = sb("weight", [P, TOPK, TT])
        slot = sb("slot", [P, TOPK, TT], I32)
        rows = sb("rows", [P, RING, TOPK, D])
        neg_half = sb("neg_half", [P, TT])
        ident = sb("ident", [P, P])
        wr = sb("wr", [D, E])
        br = sb("br", [P, E])
        before = sb("before", [P, P], BF16)
        ones_bf = sb("ones_bf", [P, P], BF16)
        e_rev = sb("e_rev", [P, TT, E])
        tile_steps = sb("tile_steps", [P, E, MAXT])
        tile_no = sb("tile_no", [P, NT, E])
        restart = sb("restart", [P, E, TT])
        ones_e = sb("ones_e", [P, E])
        lane = sb("lane", [P, P])
        block_no = sb("block_no", [P, BLOCKS])
        token_no = sb("token_no", [P, TT])
        w_all = sb("w_all", [P, E, WROW])
        wqkv = sb("wqkv", [D, 3, D])
        wo = sb("wo", [P, G, D])
        bqk = sb("bqk", [P, 2])
        bvo = sb("bvo", [P, 2, D])
        spread = sb("spread", [P, P])
        qk_rows = nc.dram_tensor("qk_rows", [2, 2, P, S], F32).ap()
        max_rows = nc.dram_tensor("max_rows", [2, J, S], F32).ap()
        qx = sb("qx", [P, G, J, S], F32R)
        kx = sb("kx", [P, G, J, S], F32R)

        with ExitStack() as ffn_only:
            def sb_ffn(name, shape, dt=F32):
                return ffn_only.enter_context(nc.sbuf_tensor(name, shape, dt))

            xnT = sb_ffn("xnT", [P, 2, BANK])
            score = sb_ffn("score", [P, TT, E])
            score2 = sb_ffn("score2", [P, TT, E])
            hit = sb_ffn("hit", [P, TT, E])
            pick = [sb_ffn(f"pick{j}", [P, TT, E]) for j in range(TOPK)]
            picked = sb_ffn("picked", [P, TT, E], BF16)
            best = [sb_ffn(f"best{j}", [P, TT]) for j in range(TOPK)]
            key = sb_ffn("key", [P, TT])
            gap = sb_ffn("gap", [P, TT])
            den = sb_ffn("den", [P, TT])
            totals = sb_ffn("totals", [P, E, TT])
            running = sb_ffn("running", [P, E, TT])
            fill = sb_ffn("fill", [P, E, MAXT])
            tiles_e = sb_ffn("tiles_e", [P, E])
            ends = sb_ffn("ends", [P, E])
            base = sb_ffn("base", [P, E])
            where = sb_ffn("where", [P, TT, E])
            where_j = sb_ffn("where_j", [P, TT, E])
            slot_f = sb_ffn("slot_f", [P, TOPK, TT])
            lane_int = sb_ffn("lane_int", [P, TOPK, TT], I32)
            block_int = sb_ffn("block_int", [P, TOPK, TT], I32)
            slot_lane = sb_ffn("slot_lane", [P, TOPK, TT])
            slot_block = sb_ffn("slot_block", [P, TOPK, TT])
            past = sb_ffn("past", [P, NT, E])
            expert_f = sb_ffn("expert_f", [P, NT])
            expert = sb_ffn("expert", [P, NT], I32)
            in_lane = sb_ffn("in_lane", [P, 2, TOPK, P])
            in_block = sb_ffn("in_block", [P, 2, TOPK, BLOCKS])
            token = sb_ffn("token", [P, BLOCKS], I32)
            w_up = sb_ffn("w_up", [P, 2, UP])
            w_down = sb_ffn("w_down", [P, 2, WROW - UP])
            xs = sb_ffn("xs", [P, AHEAD, SB, D])
            xsT = sb_ffn("xsT", [P, 2, SLOTS])
            hT = sb_ffn("hT", [P, 2, HC, SLOTS])
            ys = sb_ffn("ys", [P, 2, SB, D])

        probs = xn[:].rearrange("p t d -> p (t d)").rearrange("p (b j s) -> p b j s", b=2, j=J)
        vx = sb("vx", [P, BT, HEADS, 32])
        v_rows = sb("v_rows", [P, BT, HEADS, HD])
        xb = sb("xb", [P, BT, D])
        xbT = sb("xbT", [P, S])
        q_parts = sb("q_parts", [P, 2, S], F32R)
        k_parts = sb("k_parts", [P, 2, S], F32R)
        neg_max = sb("neg_max", [P, 2, J, BT])
        max_parts = sb("max_parts", [J, 2, S], F32R)
        acc_sb = sb("acc_sb", [P, 2, S])
        recip = sb("recip", [P, S])
        attn = sb("attn", [P, G, S])

        consts = sem("consts")
        sp_waited = sem("sp_waited")
        pool_waited = sem("pool_waited")
        at_consts = sem("at_consts")
        at_loaded = sem("at_loaded")
        wo_zero = sem("wo_zero")
        xb_ready = sem("xb_ready")
        xbT_ps = sem("xbT_ps")
        xbT_sb = sem("xbT_sb")
        qk_ps = sem("qk_ps")
        qk_high = sem("qk_high")
        qk_low = sem("qk_low")
        v_ps = sem("v_ps")
        v_sb = sem("v_sb")
        vx_ready = sem("vx_ready")
        bo_added = sem("bo_added")
        qk_stored = [sem(f"{n}_stored") for n in "qk"]
        qkx_in = [sem(f"qkx_in{g}") for g in range(G)]
        max_stored = sem("max_stored")
        max_in = [sem(f"max_in{g}") for g in range(G)]
        s_ps = sem("s_ps")
        s_max = sem("s_max")
        maxT_ps = sem("maxT_ps")
        max_sb = sem("max_sb")
        st_ps = sem("st_ps")
        exp_sb = sem("exp_sb")
        pv_ps = sem("pv_ps")
        acc_out = sem("acc_out")
        den_ps = sem("den_ps")
        recip_sb = sem("recip_sb")
        attn_sb = sem("attn_sb")
        o_ps = sem("o_ps")
        o_sb = sem("o_sb")
        max_high = sem("max_high")
        x_loaded = sem("x_loaded")
        experts_in = sem("experts_in")
        xn_out = sem("xn_out")
        dve_step = sem("dve_step")
        pool_step = sem("pool_step")
        var_ready = sem("var_ready")
        rstd_ready = sem("rstd_ready")
        xn_ready = sem("xn_ready")
        xnT_ps = sem("xnT_ps")
        xnT_sb = sem("xnT_sb")
        routed_ps = sem("routed_ps")
        gap_ready = sem("gap_ready")
        gap_exp = sem("gap_exp")
        picked_ready = sem("picked_ready")
        counts_ps = sem("counts_ps")
        slots_ready = sem("slots_ready")
        one_hot = sem("one_hot")
        slot_map_ps = sem("slot_map_ps")
        tokens_ready = sem("tokens_ready")
        w_up_sb = sem("w_up_sb")
        w_down_sb = sem("w_down_sb")
        xs_in = [sem(f"xs_in{i}") for i in range(AHEAD)]
        xsT_ps = sem("xsT_ps")
        xsT_sb = sem("xsT_sb")
        h_ps = sem("h_ps")
        h_act = sem("h_act")
        h_dve = sem("h_dve")
        y_ps = sem("y_ps")
        y_sb = sem("y_sb")
        y_out = [sem(f"y_out{i}") for i in range(2)]
        gathered = [sem(f"gathered{i}") for i in range(RING)]
        combined = sem("combined")
        stored = sem("stored")

        ps_st = [psum[:, 2 * i:2 * i + 2, :] for i in range(2)]
        ps_s = [psum[:, 4 + i, :] for i in range(2)]
        ps_acc = psum[:, 6, :]
        ps_spare = psum[:, 7, :]
        ps_t = [psum[:, 6 + i, :] for i in range(2)]
        ps_slot_map = psum[:, 2, 0:BLOCKS]
        ps_h = [psum[:, 2 * i:2 * i + 2, :].rearrange("p a (b n) -> p (a b) n", b=2) for i in range(2)]
        ps_y = [psum[:, 4 + i, 0:SB * D].rearrange("p (s d) -> p s d", s=SB) for i in range(2)]
        ps_score = psum[:, 5, 0:TT * E].rearrange("p (t e) -> p t e", e=E)
        ps_rank = psum[:, 0, 0:TT * E].rearrange("p (t e) -> p t e", e=E)
        ps_total = psum[:, 1, 0:TT * E].rearrange("p (t e) -> p t e", e=E)

        xn_rows_v = xn_rows.rearrange("(t p) d -> p t d", p=P)
        slots_y_v = slots_y.rearrange("(n s p) d -> n p s d", p=P, s=SB)
        x_v = x_in.rearrange("(t p) d -> p t d", p=P)
        out_v = out.rearrange("(t p) d -> p t d", p=P)
        PHASES = 2
        QKX = 16 * 5

        def one(i):
            return bass.ds(i, 1)

        def wait(eng, semaphore, count):
            if not isinstance(count, int) or count > 0:
                eng.wait_ge(semaphore, count)

        def wait_alone(eng, semaphore, count, carrier=sp_waited):
            if not isinstance(count, int) or count > 0:
                eng.wait_ge(semaphore, count)
                eng.sem_inc(carrier, 1)

        def sequences(eng, run):
            run(0, True, False)
            with eng.Fori(1, NB - 1) as b:
                run(b, False, False)
            run(NB - 1, False, True)

        def tasks(g, c, first, last):
            what = SPARE.get((g, c))
            if last and (what in ("turn_x", "q", "k", "v") or (what == "turn_max" and g == G - 1)):
                return None
            if first and (what == "project" or (what == "spread_den" and g == 0)):
                return None
            return what

        def done(n):
            return n + 3

        def tile_of(p, i, k):
            return p * NT + 4 * i + k, (p * NT + k) % 2

        def gathers_of(p, k):
            return p * ((NT + AHEAD - 1 - k) // AHEAD)

        def tiles(eng, step):
            with eng.Fori(0, (NT - 2) // 4) as i:
                for k in range(4):
                    step(i, k, True, True)
            for n in range((NT - 2) // 4 * 4, NT):
                step(n // 4, n % 4, n + 1 < NT, n + 2 < NT)

        block = ctx.enter_context(nc.Block())

        @block.gpsimd
        def _(pool):
            n = [0]

            def step(ins):
                ins.then_inc(pool_step, 1)
                n[0] += 1
                pool.wait_ge(pool_step, n[0])

            step(nc.gpsimd.memset(ident[:], 0.0))
            step(nc.gpsimd.memset(before[:], 1.0))
            step(nc.gpsimd.affine_select(out=ident[:], in_=ident[:], compare_op=ALU.not_equal, fill=1.0,
                                         base=0, pattern=[[-1, P]], channel_multiplier=1))
            step(nc.gpsimd.affine_select(out=before[:], in_=before[:], compare_op=ALU.is_gt, fill=0.0,
                                         base=0, pattern=[[1, P]], channel_multiplier=-1))
            step(nc.gpsimd.memset(ones_bf[:], 1.0))
            step(nc.gpsimd.memset(neg_half[:], -0.5))
            step(nc.gpsimd.memset(ones_e[:], 1.0))
            step(nc.gpsimd.memset(restart[:], 1.0))
            step(nc.gpsimd.memset(restart[:, :, 0:1], 0.0))
            step(nc.gpsimd.iota(e_rev[:], [[0, TT], [-1, E]], base=E, channel_multiplier=0,
                                allow_small_or_imprecise_dtypes=True))
            step(nc.gpsimd.iota(tile_steps[:], [[0, E], [SLOTS, MAXT]], base=0, channel_multiplier=0,
                                allow_small_or_imprecise_dtypes=True))
            nc.gpsimd.iota(tile_no[:], [[1, NT], [0, E]], base=0, channel_multiplier=0,
                           allow_small_or_imprecise_dtypes=True).then_inc(pool_step, 1)
            n[0] += 1
            pool.wait_ge(pool_step, n[0])
            step(nc.gpsimd.iota(lane[:], [[1, P]], base=0, channel_multiplier=0, allow_small_or_imprecise_dtypes=True))
            step(nc.gpsimd.iota(block_no[:], [[1, BLOCKS]], base=0, channel_multiplier=0,
                                allow_small_or_imprecise_dtypes=True))
            nc.gpsimd.iota(token_no[:], [[P, TT]], base=0, channel_multiplier=1,
                           allow_small_or_imprecise_dtypes=True).then_inc(consts, 1)
            def attention_consts():
                step(nc.gpsimd.memset(spread[:], 0.0))
                step(nc.gpsimd.affine_select(out=spread[:].rearrange("p (j r) -> p j r", j=J), in_=spread[:].rearrange("p (j r) -> p j r", j=J),
                                             compare_op=ALU.not_equal, fill=1.0, base=-DEN, pattern=[[-32, J], [0, 32]],
                                             channel_multiplier=1))
                step(nc.gpsimd.memset(qx[:].bitcast(F32), 0.0))
                step(nc.gpsimd.memset(kx[:].bitcast(F32), 0.0))
                nc.gpsimd.memset(kx[SHIFT:SHIFT + 2].bitcast(F32), 1.0).then_inc(at_consts, 1)
                pool.wait_ge(at_consts, 1)

            def expand_v(b, g):
                wait_alone(pool, pv_ps, 16 * b - 16 + 4 * g + 4, pool_waited)
                wait_alone(pool, v_sb, b + 1, pool_waited)
                nc.gpsimd.tensor_copy(vx[:, :, J * g:J * g + J, 0:HD], v_rows[:, :, J * g:J * g + J, :]).then_inc(vx_ready, 1)

            def normalize(b, g):
                u = 4 * b + g
                pool.wait_ge(recip_sb, u + 1)
                wait(pool, o_ps, b)
                nc.gpsimd.tensor_tensor(attn[:, g, :], acc_sb[:, g % 2, :], recip[:], ALU.mult).then_inc(attn_sb, 1)

            def add_bo(b):
                pool.wait_ge(xb_ready, b + 1)
                nc.gpsimd.tensor_tensor(x[:, bass.ds(4 * b, BT), :], x[:, bass.ds(4 * b, BT), :],
                                        bvo[:, 1:2, :].to_broadcast([P, BT, D]), ALU.add).then_inc(bo_added, 1)

            def attention():
                step(nc.gpsimd.memset(vx[:], 0.0))
                step(nc.gpsimd.memset(vx[:, :, :, DEN:DEN + 1], 1.0))
                add_bo(0)
                for g in range(G):
                    expand_v(0, g)

                def run(b, first, last):
                    if not first:
                        normalize(b - 1, G - 1)
                        expand_v(b, G - 1)
                    if not last:
                        add_bo(b + 1)
                    for g in range(1, G):
                        normalize(b, g - 1)
                    if not last:
                        for g in range(G - 1):
                            expand_v(b + 1, g)

                sequences(pool, run)
                normalize(NB - 1, G - 1)

            for p in range(PHASES):
                if p == 1:
                    pool.wait_ge(var_ready, 2)
                    nc.gpsimd.tensor_tensor(rstd[:], var_eps[:], neg_half[:], ALU.pow).then_inc(rstd_ready, 1)
                    pool.wait_ge(at_loaded, 16 * (3 + J))
                    attention()
                pool.wait_ge(var_ready, 2 * p + 1)
                nc.gpsimd.tensor_tensor(rstd[:], var_eps[:], neg_half[:], ALU.pow).then_inc(rstd_ready, 1)
                if p == 0:
                    attention_consts()
                pool.wait_ge(xn_out, 16 * (TT // 4) * (p + 1))
                pool.wait_ge(tokens_ready, p + 1)
                for t in range(NT):
                    if t < AHEAD:
                        if p:
                            pool.wait_ge(xsT_ps, done(p * NT - 1))
                    else:
                        pool.wait_ge(xsT_ps, done(p * NT + t - AHEAD))
                    for s in range(SB):
                        at = SB * t + s
                        nc.gpsimd.indirect_dma_start(
                            xs[:, t % AHEAD, s, :], None, xn_rows,
                            bass.IndirectOffsetOnAxis(ap=token[:, at:at + 1], axis=0)).then_inc(xs_in[t % AHEAD], 16)
                for k in range(2):
                    pool.wait_ge(y_out[k], 16 * (((p + 1) * NT + 1 - k) // 2 + 1))
                for t in range(TT):
                    g = p * TT + t
                    if g >= RING:
                        pool.wait_ge(combined, g - RING + 1)
                    for j in range(TOPK):
                        nc.gpsimd.indirect_dma_start(
                            rows[:, g % RING, j, :], None, slots_y,
                            bass.IndirectOffsetOnAxis(ap=slot[:, j, t:t + 1], axis=0)).then_inc(gathered[g % RING], 16)

        @block.sync
        def _(sp):
            sp.dma_start(x[:], x_v).then_inc(x_loaded, 16)
            sp.dma_start(wr[:], wr_in).then_inc(x_loaded, 16)
            sp.dma_start(br[:], br_in.partition_broadcast(P)).then_inc(x_loaded, 16)
            for e in range(E):
                sp.dma_start(w_all[:, e, :], experts[e]).then_inc(experts_in, 16)
            sp.dma_start(wqkv[:], wqkv_in).then_inc(at_loaded, 16)
            sp.dma_start(bqk[:], bqk_in).then_inc(at_loaded, 16)
            sp.dma_start(bvo[:], bvo_in.partition_broadcast(P)).then_inc(at_loaded, 16)
            sp.wait_ge(wo_zero, 1)
            wo_v = wo_in.rearrange("(g j r) n -> j r g n", g=G, j=J)
            for j in range(J):
                sp.dma_start(wo[32 * j:32 * j + HD, :, :], wo_v[j]).then_inc(at_loaded, 16)

            def store_qk(b, which):
                wait_alone(sp, qk_low, 2 * b + which + 1)
                for g in range(G):
                    wait_alone(sp, qkx_in[g], QKX * b)
                parts = (q_parts, k_parts)[which]
                sp.dma_start(qk_rows[which].rearrange("h p n -> p h n"), parts[:].bitcast(F32)).then_inc(qk_stored[which], 16)

            def expand_qk(b, g):
                for s in qk_stored:
                    wait_alone(sp, s, 16 * (b + 1))
                wait_alone(sp, st_ps, 32 * b - 32 + 8 * g + 8)
                q_of, k_of = (qk_rows[i].rearrange("h (d g j) n -> g h d (j n)", d=HD, g=G)[g] for i in range(2))
                for h in range(2):
                    sp.dma_start(qx[2 * HD * h:2 * HD * (h + 1), g, :, :].rearrange("p j n -> p (j n)").bitcast(F32),
                                 q_of[h].unsqueeze(0).to_broadcast([2, HD, J * S])).then_inc(qkx_in[g], 16)
                for r in range(2):
                    sp.dma_start(kx[2 * HD * r:2 * HD * (r + 1), g, :, :].rearrange("p j n -> p (j n)").bitcast(F32), k_of).then_inc(qkx_in[g], 16)
                sp.dma_start(qx[SHIFT:SHIFT + 2, g, :, :].rearrange("p j n -> p (j n)").bitcast(F32),
                             qx[SHIFT + 2:SHIFT + 4, g, :, :].rearrange("p j n -> p (j n)").bitcast(F32)).then_inc(qkx_in[g], 16)

            def place_max(b, g):
                u = 4 * b + g
                wait_alone(sp, max_sb, u + 1)
                if g:
                    wait_alone(sp, max_in[g - 1], 16 * (b + 1))
                else:
                    wait_alone(sp, max_in[G - 1], 16 * b)
                sp.dma_start(max_rows.rearrange("h j n -> j h n"), max_parts[:].bitcast(F32)).then_inc(max_stored, 16)
                wait_alone(sp, max_stored, 16 * (u + 1))
                sp.dma_start(qx[SHIFT:SHIFT + 2, g, :, :].rearrange("p j n -> p (j n)").bitcast(F32),
                             max_rows.rearrange("h j n -> h (j n)")).then_inc(max_in[g], 16)

            def attention():
                store_qk(0, 0)
                store_qk(0, 1)
                for g in range(G - 1):
                    expand_qk(0, g)
                place_max(0, 0)

                def run(b, first, last):
                    expand_qk(b, G - 1)
                    place_max(b, 1)
                    if not last:
                        store_qk(b + 1, 0)
                        store_qk(b + 1, 1)
                        expand_qk(b + 1, 0)
                    place_max(b, 2)
                    if not last:
                        expand_qk(b + 1, 1)
                    place_max(b, 3)
                    if not last:
                        expand_qk(b + 1, 2)
                        place_max(b + 1, 0)

                sequences(sp, run)

            for p in range(PHASES):
                if p == 1:
                    sp.wait_ge(at_consts, 1)
                    attention()
                for q in range(TT // 4):
                    sp.wait_ge(xn_ready, p * (TT // 4) + q + 1)
                    sp.dma_start(xn_rows_v[:, 4 * q:4 * q + 4, :], xn[:, 4 * q:4 * q + 4, :]).then_inc(xn_out, 16)
            for q in range(TT // 4):
                sp.wait_ge(combined, TT + 4 * q + 4)
                sp.dma_start(out_v[:, 4 * q:4 * q + 4, :], x[:, 4 * q:4 * q + 4, :]).then_inc(stored, 16)
            sp.wait_ge(stored, 16 * (TT // 4))

        @block.scalar
        def _(act):
            def front(p):
                with act.Fori(0, TT // 8) as i:
                    for k in range(2):
                        g = p * (TT // 4) + 2 * i + k
                        act.wait_ge(xnT_ps, g + 1)
                        act.wait_ge(routed_ps, done(g - 2))
                        nc.scalar.activation(xnT[:, k, :], ps_t[0], ACT.Copy).then_inc(xnT_sb, 1)
                act.wait_ge(gap_ready, p + 1)
                nc.scalar.activation(gap[:], gap[:], ACT.Exp).then_inc(gap_exp, 1)

            def fetch_up(p, i, k):
                n, b = tile_of(p, i, k)
                e = act.value_load(expert[0:1, one(4 * i + k)], min_val=0, max_val=E - 1)
                act.wait_ge(h_ps, done(n - 2))
                act.wait_ge(h_dve, done(n - 2))
                act.wait_ge(h_act, done(n - 2))
                nc.scalar.activation(w_up[:, b, :], w_all[:, one(e), 0:UP], ACT.Copy).then_inc(w_up_sb, 1)

            def fetch_down(p, i, k):
                n, b = tile_of(p, i, k)
                e = act.value_load(expert[0:1, one(4 * i + k)], min_val=0, max_val=E - 1)
                act.wait_ge(y_sb, done(n - 2))
                nc.scalar.activation(w_down[:, b, :], w_all[:, one(e), UP:WROW], ACT.Copy).then_inc(w_down_sb, 1)

            def hidden(p, i, k):
                n, b = tile_of(p, i, k)
                act.wait_ge(h_ps, done(n))
                act.wait_ge(y_ps, done(n - 2))
                for c in range(HC // 2):
                    last = nc.scalar.activation(hT[:, b, c, :], ps_h[b][:, c, :], ACT.Relu, bias=w_up[:, b, H + c:H + c + 1])
                last.then_inc(h_act, 1)

            def store(p, i, k):
                n, b = tile_of(p, i, k)
                act.wait_ge(y_sb, done(n))
                act.dma_start(slots_y_v[one(4 * i + k)].rearrange("n p s d -> p (n s) d"), ys[:, b, :, :]).then_inc(y_out[b], 16)

            def turn_x_out(b):
                act.wait_ge(xbT_ps, b + 1)
                wait(act, v_ps, b)
                nc.scalar.activation(xbT[:], ps_spare, ACT.Copy).then_inc(xbT_sb, 1)

            def high(b, which):
                act.wait_ge(qk_ps, 2 * b + which + 1)
                wait(act, qk_stored[which], 16 * b)
                parts = (q_parts, k_parts)[which]
                nc.scalar.activation(parts[:, 0, :], ps_spare, ACT.Identity, bias=bqk[:, which:which + 1]).then_inc(qk_high, 1)

            def exps(b, g, c, half):
                step = 16 * b + 4 * g + c
                act.wait_ge(st_ps, 2 * step + half + 1)
                wait(act, pv_ps, step - 1)
                nc.scalar.activation(probs[:, c % 2, 2 * half:2 * half + 2, :], ps_st[half], ACT.Exp,
                                     scale=HD ** -0.5).then_inc(exp_sb, 1)

            def acc_done(b, g):
                u = 4 * b + g
                act.wait_ge(pv_ps, 4 * u + 4)
                wait(act, attn_sb, u - 1)
                nc.scalar.activation(acc_sb[:, g % 2, :], ps_acc, ACT.Copy).then_inc(acc_out, 1)

            def attention():
                turn_x_out(0)
                high(0, 0)
                high(0, 1)

                def run(b, first, last):
                    for g in range(G):
                        for c in range(BT):
                            exps(b, g, c, 0)
                            what = tasks(g, c - 1, first, last) if c else tasks(g - 1, BT - 1, first, last)
                            if what == "turn_x":
                                turn_x_out(b + 1)
                            elif what == "q":
                                high(b + 1, 0)
                            elif what == "k":
                                high(b + 1, 1)
                            exps(b, g, c, 1)
                            if c == 0 and not (first and g == 0):
                                acc_done(b - (g == 0), (g - 1) % G)

                sequences(act, run)
                acc_done(NB - 1, G - 1)

            for s in (xnT_sb, h_act, w_up_sb, w_down_sb):
                act.sem_inc(s, 2)
            for s in y_out:
                act.sem_inc(s, 16)
            for p in range(PHASES):
                if p == 1:
                    attention()
                front(p)
                act.wait_ge(slots_ready, p + 1)
                if p == 0:
                    act.wait_ge(experts_in, 16 * E)
                fetch_up(p, 0, 0)
                fetch_down(p, 0, 0)
                fetch_up(p, 0, 1)
                hidden(p, 0, 0)

                def step(i, k, up1, up2):
                    if up1:
                        fetch_down(p, i, k + 1)
                    if up2:
                        fetch_up(p, i, k + 2)
                    if up1:
                        hidden(p, i, k + 1)
                    store(p, i, k)

                tiles(act, step)

        @block.tensor
        def _(pe):
            for s in (routed_ps, slot_map_ps, xsT_ps, h_ps, y_ps):
                pe.sem_inc(s, 2)

            def front(p):
                for q in range(TT // 4):
                    g = p * (TT // 4) + q
                    pe.wait_ge(xn_ready, g + 1)
                    pe.wait_ge(xnT_sb, done(g - 1))
                    for j in range(4):
                        mm = nc.tensor.transpose(ps_t[0][:, j * P:(j + 1) * P], xn[:, 4 * q + j, :], ident[:])
                    mm.then_inc(xnT_ps, 1)
                    pe.wait_ge(xnT_sb, done(g))
                    for j in range(4):
                        mm = nc.tensor.matmul(ps_score[:, 4 * q + j, :], xnT[:, q % 2, j * P:(j + 1) * P], wr[:],
                                              start=True, stop=True)
                    mm.then_inc(routed_ps, 1)
                pe.wait_ge(picked_ready, p + 1)
                rhs = picked[:].rearrange("p t e -> p (t e)")
                nc.tensor.matmul(psum[:, 0, 0:TT * E], before[:], rhs, start=True, stop=True)
                nc.tensor.matmul(psum[:, 1, 0:TT * E], ones_bf[:], rhs, start=True, stop=True).then_inc(counts_ps, 1)
                for t in range(TT):
                    pe.wait_ge(one_hot, done(p * TT + t))
                    for j in range(TOPK):
                        mm = nc.tensor.matmul(ps_slot_map, in_lane[:, t % 2, j, :], in_block[:, t % 2, j, :],
                                              start=(t == 0 and j == 0), stop=(t == TT - 1 and j == TOPK - 1))
                    mm.then_inc(slot_map_ps, 1)

            def turn(p, i, k):
                n, b = tile_of(p, i, k)
                pe.wait_ge(xs_in[k % AHEAD], 16 * SB * (gathers_of(p, k % AHEAD) + i + k // AHEAD + 1))
                pe.wait_ge(xsT_sb, done(n - 2))
                for s in range(SB):
                    mm = nc.tensor.transpose(ps_t[b][:, s * P:(s + 1) * P], xs[:, k % AHEAD, s, :], ident[:])
                mm.then_inc(xsT_ps, 1)

            def up(p, i, k):
                n, b = tile_of(p, i, k)
                pe.wait_ge(xsT_sb, done(n))
                pe.wait_ge(w_up_sb, done(n))
                pe.wait_ge(h_act, done(n - 2))
                pe.wait_ge(h_dve, done(n - 2))
                for c in range(HC):
                    mm = nc.tensor.matmul(ps_h[b][:, c, :], w_up[:, b, c * P:(c + 1) * P], xsT[:, b, :],
                                          start=True, stop=True)
                mm.then_inc(h_ps, 1)

            def down(p, i, k):
                n, b = tile_of(p, i, k)
                pe.wait_ge(h_act, done(n))
                pe.wait_ge(h_dve, done(n))
                pe.wait_ge(w_down_sb, done(n))
                pe.wait_ge(y_sb, done(n - 2))
                for s in range(SB):
                    for c in range(HC):
                        mm = nc.tensor.matmul(ps_y[b][:, s, :], hT[:, b, c, s * P:(s + 1) * P],
                                              w_down[:, b, c * D:(c + 1) * D], start=(c == 0), stop=(c == HC - 1))
                mm.then_inc(y_ps, 1)

            def turn_x(b):
                pe.wait_ge(xb_ready, b + 1)
                for j in range(BT):
                    mm = nc.tensor.transpose(ps_spare[:, j * P:(j + 1) * P], xb[:, j, :], ident[:])
                mm.then_inc(xbT_ps, 1)

            def project_qk(b, which):
                pe.wait_ge(xbT_sb, b + 1)
                nc.tensor.matmul(ps_spare, wqkv[:, which, :], xbT[:], start=True, stop=True).then_inc(qk_ps, 1)

            def project_v(b):
                for j in range(BT):
                    mm = nc.tensor.matmul(ps_spare[:, j * P:(j + 1) * P], xbT[:, j * P:(j + 1) * P], wqkv[:, 2, :],
                                          start=True, stop=True)
                mm.then_inc(v_ps, 1)

            def project_out(b):
                pe.wait_ge(attn_sb, 4 * b + 4)
                for j in range(BT):
                    for g in range(G):
                        mm = nc.tensor.matmul(ps_spare[:, j * P:(j + 1) * P], attn[:, g, j * P:(j + 1) * P], wo[:, g, :],
                                              start=(g == 0), stop=(g == G - 1))
                mm.then_inc(o_ps, 1)

            def turn_max(b, g):
                pe.wait_ge(s_max, 16 * (4 * b + g) + 16)
                for c in range(BT):
                    mm = nc.tensor.transpose(ps_spare[0:J, c * P:(c + 1) * P], neg_max[:, g % 2, :, c], ident[:])
                mm.then_inc(maxT_ps, 1)

            def spread_den(b, g):
                pe.wait_ge(acc_out, 4 * b + g + 1)
                nc.tensor.matmul(ps_spare, spread[:], acc_sb[:, g % 2, :], start=True, stop=True).then_inc(den_ps, 1)

            def scores(b, g, j, c):
                if j == 0 and c == 0:
                    pe.wait_ge(qkx_in[g], QKX * (b + 1))
                block = 16 * (4 * b + g) + 4 * j + c
                wait(pe, s_max, block - 1)
                nc.tensor.matmul(ps_s[c % 2], qx[:, g, j, c * P:(c + 1) * P], kx[:, g, j, :],
                                 start=True, stop=True).then_inc(s_ps, 1)

            def shifted(b, g, c, half):
                if c == 0 and half == 0:
                    pe.wait_ge(max_in[g], 16 * (b + 1))
                wait(pe, exp_sb, 2 * (16 * b + 4 * g + c) + half - 1)
                for i in range(2):
                    j = 2 * half + i
                    mm = nc.tensor.matmul(ps_st[half][:, i, :], kx[:, g, j, c * P:(c + 1) * P], qx[:, g, j, :],
                                          start=True, stop=True)
                mm.then_inc(st_ps, 1)

            def values(b, g, c):
                u = 4 * b + g
                pe.wait_ge(exp_sb, 2 * (4 * u + c) + 2)
                if c == 0:
                    pe.wait_ge(vx_ready, u + 1)
                    wait(pe, acc_out, u)
                for j in range(J):
                    mm = nc.tensor.matmul(ps_acc[32 * j:32 * j + 32, :], vx[:, c, J * g + j, :], probs[:, c % 2, j, :],
                                          start=(c == 0), stop=(c == BT - 1))
                mm.then_inc(pv_ps, 1)

            def attention():
                pe.wait_ge(at_loaded, 16 * (3 + J))
                pe.wait_ge(at_consts, 1)
                turn_x(0)
                project_qk(0, 0)
                pe.wait_ge(qk_low, 1)
                project_qk(0, 1)
                pe.wait_ge(qk_low, 2)
                project_v(0)
                for u in range(2):
                    for j in range(J):
                        for c in range(BT):
                            scores(0, u, j, c)
                pe.wait_ge(v_sb, 1)
                turn_max(0, 0)

                def run(b, first, last):
                    for g in range(G):
                        ahead = not (last and g >= 2)
                        for c in range(BT):
                            for half in range(2):
                                shifted(b, g, c, half)
                                if ahead:
                                    for i in range(2):
                                        scores(b + (g + 2) // G, (g + 2) % G, c, 2 * half + i)
                            if c:
                                values(b, g, c - 1)
                            elif not (first and g == 0):
                                values(b - (g == 0), (g - 1) % G, BT - 1)
                            spare_task(b, g, c, first, last)

                sequences(pe, run)
                values(NB - 1, G - 1, BT - 1)
                pe.wait_ge(recip_sb, 4 * NB - 1)
                spread_den(NB - 1, G - 1)
                pe.wait_ge(recip_sb, 4 * NB)
                project_out(NB - 1)

            def spare_task(b, g, c, first, last):
                what = tasks(g, c, first, last)
                before = None
                at = 4 * g + c - 1
                while what and before is None and at >= 0:
                    before = tasks(at // 4, at % 4, first, last)
                    at -= 1
                if before is None and what:
                    wait(pe, recip_sb, 4 * b - 1)
                    if first:
                        pe.wait_ge(max_sb, 1)
                    bg = 0
                elif what:
                    bg = (at + 1) // 4
                if before == "turn_max":
                    pe.wait_ge(max_sb, 4 * b + bg + 2)
                elif before == "spread_den":
                    pe.wait_ge(recip_sb, 4 * b + bg)
                elif before == "turn_x":
                    pe.wait_ge(xbT_sb, b + 2)
                elif before == "q":
                    pe.wait_ge(qk_low, 2 * b + 3)
                elif before == "k":
                    pe.wait_ge(qk_low, 2 * b + 4)
                elif before == "project":
                    pe.wait_ge(o_sb, b)
                elif before == "v":
                    pe.wait_ge(v_sb, b + 2)
                if what == "turn_max":
                    turn_max(b + (g + 1) // G, (g + 1) % G)
                elif what == "spread_den":
                    spread_den(b - (g == 0), (g - 1) % G)
                elif what == "turn_x":
                    turn_x(b + 1)
                elif what == "q":
                    project_qk(b + 1, 0)
                elif what == "k":
                    project_qk(b + 1, 1)
                elif what == "v":
                    project_v(b + 1)
                elif what == "project":
                    project_out(b - 1)

            pe.wait_ge(consts, 1)
            pe.wait_ge(x_loaded, 48)
            for p in range(PHASES):
                if p == 1:
                    attention()
                front(p)
                turn(p, 0, 0)
                turn(p, 0, 1)
                up(p, 0, 0)

                def step(i, k, up1, up2):
                    if up2:
                        turn(p, i, k + 2)
                    if up1:
                        up(p, i, k + 1)
                    down(p, i, k)

                tiles(pe, step)

        @block.vector
        def _(dve):
            n = [0]

            def step(ins):
                ins.then_inc(dve_step, 1)
                n[0] += 1
                dve.wait_ge(dve_step, n[0])

            nc.vector.memset(wo[:], 0.0).then_inc(wo_zero, 1)
            for s in (h_dve, y_sb, xsT_sb, one_hot):
                dve.sem_inc(s, 2)
            dve.wait_ge(x_loaded, 48)
            dve.wait_ge(consts, 1)

            def statistics(k):
                for t in range(TT):
                    last = nc.vector.bn_stats(stats[:, t, :], x[:, t, :])
                step(last)
                for t in range(TT):
                    last = nc.vector.bn_aggr(meanvar[:, t, :], stats[:, t, :])
                step(last)
                nc.vector.tensor_scalar(var_eps[:], meanvar[:, :, 1], EPS, None, ALU.add).then_inc(var_ready, 1)
                dve.wait_ge(rstd_ready, k + 1)

            def front(p):
                statistics(2 * p)
                with dve.Fori(0, TT // 4) as i:
                    for j in range(4):
                        last = nc.vector.tensor_scalar(
                            xn[:, one(4 * i + j), :], x[:, one(4 * i + j), :],
                            meanvar[:, one(4 * i + j), 0], rstd[:, one(4 * i + j)], ALU.subtract, ALU.mult)
                    last.then_inc(xn_ready, 1)

            def route(p):
                def over_e(ap):
                    return ap.unsqueeze(2).to_broadcast([P, TT, E])

                dve.wait_ge(routed_ps, done((p + 1) * (TT // 4) - 1))
                step(nc.vector.tensor_tensor(score[:], ps_score, br[:].unsqueeze(1).to_broadcast([P, TT, E]), ALU.add))
                for j in range(TOPK):
                    s = score if j == 0 else score2
                    step(nc.vector.tensor_reduce(best[j][:], s[:], AX.X, ALU.max))
                    step(nc.vector.tensor_tensor(hit[:], s[:], over_e(best[j][:]), ALU.is_equal))
                    step(nc.vector.tensor_tensor(hit[:], hit[:], e_rev[:], ALU.mult))
                    step(nc.vector.tensor_reduce(key[:], hit[:], AX.X, ALU.max))
                    step(nc.vector.tensor_tensor(pick[j][:], e_rev[:], over_e(key[:]), ALU.is_equal))
                    if j == 0:
                        step(nc.vector.scalar_tensor_tensor(score2[:], pick[0][:], -3e38, score[:], ALU.mult, ALU.add))
                nc.vector.tensor_tensor(picked[:], pick[0][:], pick[1][:], ALU.add).then_inc(picked_ready, 1)
                nc.vector.tensor_tensor(gap[:], best[1][:], best[0][:], ALU.subtract).then_inc(gap_ready, 1)
                dve.wait_ge(gap_exp, p + 1)
                step(nc.vector.tensor_scalar(den[:], gap[:], 1.0, None, ALU.add))
                step(nc.vector.reciprocal(den[:], den[:]))
                step(nc.vector.tensor_scalar(weight[:, 0, :], den[:], 0.5, None, ALU.mult))
                step(nc.vector.tensor_tensor(weight[:, 1, :], weight[:, 0, :], gap[:], ALU.mult))
                dve.wait_ge(counts_ps, p + 1)
                step(nc.vector.tensor_copy(totals[:], ps_total.rearrange("p t e -> p e t")))
                step(nc.vector.tensor_tensor_scan(running[:].rearrange("p e t -> p (e t)"), restart[:].rearrange("p e t -> p (e t)"),
                                                  totals[:].rearrange("p e t -> p (e t)"), 0.0, ALU.mult, ALU.add))
                step(nc.vector.tensor_tensor(fill[:], running[:, :, TT - 1:TT].to_broadcast([P, E, MAXT]), tile_steps[:], ALU.is_gt))
                step(nc.vector.tensor_reduce(tiles_e[:], fill[:], AX.X, ALU.add))
                step(nc.vector.tensor_tensor_scan(ends[:], ones_e[:], tiles_e[:], 0.0, ALU.mult, ALU.add))
                step(nc.vector.tensor_tensor(base[:], ends[:], tiles_e[:], ALU.subtract))
                step(nc.vector.tensor_scalar(base[:], base[:], float(SLOTS), None, ALU.mult))
                step(nc.vector.tensor_tensor(running[:], running[:], totals[:], ALU.subtract))
                step(nc.vector.tensor_tensor(running[:], running[:], base[:].unsqueeze(2).to_broadcast([P, E, TT]), ALU.add))
                step(nc.vector.tensor_tensor(where[:], ps_rank, running[:].rearrange("p e t -> p t e"), ALU.add))
                for j in range(TOPK):
                    step(nc.vector.tensor_tensor(where_j[:], where[:], pick[j][:], ALU.mult))
                    step(nc.vector.tensor_reduce(slot_f[:, j, :], where_j[:], AX.X, ALU.add))
                step(nc.vector.tensor_copy(slot[:], slot_f[:]))
                nc.vector.tensor_scalar(lane_int[:], slot[:], P - 1, None, ALU.bitwise_and)
                step(nc.vector.tensor_scalar(block_int[:], slot[:], P.bit_length() - 1, None, ALU.logical_shift_right))
                nc.vector.tensor_copy(slot_lane[:], lane_int[:])
                nc.vector.tensor_copy(slot_block[:], block_int[:])
                step(nc.vector.tensor_tensor(past[:], tile_no[:], ends[:].unsqueeze(1).to_broadcast([P, NT, E]), ALU.is_ge))
                step(nc.vector.tensor_reduce(expert_f[:], past[:], AX.X, ALU.add))
                nc.vector.tensor_scalar(expert[:], expert_f[:], float(E - 1), None, ALU.min).then_inc(slots_ready, 1)

            def slot_map(p):
                dve.wait_ge(slots_ready, p + 1)
                with dve.Fori(0, TT // 2) as i:
                    for k in range(2):
                        t = 2 * i + k
                        dve.wait_ge(slot_map_ps, done(p * TT + t - 2))
                        for j in range(TOPK):
                            nc.vector.tensor_scalar(in_lane[:, k, j, :], lane[:], slot_lane[:, j, one(t)], None, ALU.is_equal)
                            last = nc.vector.tensor_scalar(in_block[:, k, j, :], block_no[:], slot_block[:, j, one(t)],
                                                           token_no[:, one(t)], ALU.is_equal, ALU.mult)
                        last.then_inc(one_hot, 1)
                dve.wait_ge(slot_map_ps, done((p + 1) * TT - 1))
                nc.vector.tensor_copy(token[:], ps_slot_map).then_inc(tokens_ready, 1)

            def turned(p, i, k):
                n, b = tile_of(p, i, k)
                dve.wait_ge(xsT_ps, done(n))
                dve.wait_ge(h_ps, done(n - 2))
                nc.vector.tensor_copy(xsT[:, b, :], ps_t[b][:, 0:SLOTS]).then_inc(xsT_sb, 1)

            def hidden(p, i, k):
                n, b = tile_of(p, i, k)
                dve.wait_ge(h_ps, done(n))
                dve.wait_ge(w_up_sb, done(n))
                dve.wait_ge(y_ps, done(n - 2))
                for c in range(HC // 2, HC):
                    last = nc.vector.tensor_scalar(hT[:, b, c, :], ps_h[b][:, c, :], w_up[:, b, H + c:H + c + 1], 0.0,
                                                   ALU.add, ALU.max)
                last.then_inc(h_dve, 1)

            def result(p, i, k):
                n, b = tile_of(p, i, k)
                dve.wait_ge(y_ps, done(n))
                dve.wait_ge(w_down_sb, done(n))
                lap = (p * NT + k) // 2 + 2 * i + 1
                dve.wait_ge(y_out[b], 16 * lap)
                nc.vector.tensor_tensor(ys[:, b, :, :], ps_y[b], w_down[:, b, B2_AT:B2_AT + D].unsqueeze(1).to_broadcast([P, SB, D]),
                                        ALU.add).then_inc(y_sb, 1)

            def combine(p):
                for t in range(TT):
                    g = p * TT + t
                    dve.wait_ge(gathered[g % RING], 32 * (g // RING + 1))
                    step(nc.vector.scalar_tensor_tensor(x[:, t, :], rows[:, g % RING, 0, :], weight[:, 0, t:t + 1], x[:, t, :],
                                                        ALU.mult, ALU.add))
                    nc.vector.scalar_tensor_tensor(x[:, t, :], rows[:, g % RING, 1, :], weight[:, 1, t:t + 1], x[:, t, :],
                                                   ALU.mult, ALU.add).then_inc(combined, 1)
                dve.wait_ge(combined, (p + 1) * TT)

            def norm_x(b):
                wait(dve, xbT_ps, b)
                for j in range(BT):
                    t = 4 * b + j
                    last = nc.vector.tensor_scalar(xb[:, j, :], x[:, one(t), :], meanvar[:, one(t), 0], rstd[:, one(t)],
                                                   ALU.subtract, ALU.mult)
                last.then_inc(xb_ready, 1)

            def low(b, which):
                dve.wait_ge(qk_high, 2 * b + which + 1)
                parts = (q_parts, k_parts)[which]
                nc.vector.scalar_tensor_tensor(parts[:, 1, :], ps_spare, bqk[:, which:which + 1], parts[:, 0, :].bitcast(F32),
                                               ALU.add, ALU.subtract).then_inc(qk_low, 1)

            def v_done(b):
                dve.wait_ge(v_ps, b + 1)
                wait(dve, vx_ready, 4 * b)
                nc.vector.tensor_tensor(v_rows[:].rearrange("p t h d -> p t (h d)"), ps_spare.rearrange("p (t n) -> p t n", t=BT),
                                        bvo[:, 0:1, :].to_broadcast([P, BT, D]), ALU.add).then_inc(v_sb, 1)

            def maximum(b, g, j, c):
                block = 16 * (4 * b + g) + 4 * j + c
                dve.wait_ge(s_ps, block + 1)
                if j == 0 and c == 0:
                    wait(dve, maxT_ps, 4 * b + g - 1)
                nc.vector.tensor_reduce(neg_max[:, g % 2, j, c:c + 1], ps_s[c % 2], AX.X, ALU.max, negate=True).then_inc(s_max, 1)

            def max_done(b, g):
                u = 4 * b + g
                dve.wait_ge(maxT_ps, u + 1)
                wait(dve, max_stored, 16 * u)
                step_counted(nc.vector.tensor_copy(max_parts[:, 0, :], ps_spare[0:J, :]), max_high, u + 1)
                nc.vector.tensor_tensor(max_parts[:, 1, :], ps_spare[0:J, :], max_parts[:, 0, :].bitcast(F32),
                                        ALU.subtract).then_inc(max_sb, 1)

            def step_counted(ins, semaphore, count):
                ins.then_inc(semaphore, 1)
                dve.wait_ge(semaphore, count)

            def den_done(b, g):
                u = 4 * b + g
                dve.wait_ge(den_ps, u + 1)
                wait(dve, attn_sb, u)
                nc.vector.reciprocal(recip[:], ps_spare).then_inc(recip_sb, 1)

            def out_done(b):
                dve.wait_ge(o_ps, b + 1)
                dve.wait_ge(bo_added, b + 1)
                xs4 = x[:, bass.ds(4 * b, BT), :]
                nc.vector.tensor_tensor(xs4, ps_spare.rearrange("p (t n) -> p t n", t=BT), xs4, ALU.add).then_inc(o_sb, 1)

            def attention():
                norm_x(0)
                low(0, 0)
                low(0, 1)
                v_done(0)
                for u in range(2):
                    for j in range(J):
                        for c in range(BT):
                            maximum(0, u, j, c)
                max_done(0, 0)

                def finish(b, g, what):
                    if what == "turn_max":
                        max_done(b + (g + 1) // G, (g + 1) % G)
                    elif what == "spread_den":
                        den_done(b - (g == 0), (g - 1) % G)
                    elif what == "q":
                        low(b + 1, 0)
                    elif what == "k":
                        low(b + 1, 1)
                    elif what == "v":
                        v_done(b + 1)
                    elif what == "project":
                        out_done(b - 1)

                def run(b, first, last):
                    for g in range(G):
                        ahead = not (last and g >= 2)
                        for c in range(BT):
                            for i in range(BT):
                                if ahead:
                                    maximum(b + (g + 2) // G, (g + 2) % G, c, i)
                                if i == 1:
                                    at = 4 * g + c - 1
                                    if at >= 0:
                                        finish(b, at // 4, tasks(at // 4, at % 4, first, last))
                                    if at == 0 and not last:
                                        norm_x(b + 1)

                sequences(dve, run)
                den_done(NB - 1, G - 1)
                out_done(NB - 1)
                dve.wait_ge(o_sb, NB)

            for p in range(PHASES):
                if p == 1:
                    statistics(1)
                    attention()
                front(p)
                route(p)
                slot_map(p)
                turned(p, 0, 0)
                turned(p, 0, 1)
                hidden(p, 0, 0)

                def tile_step(i, k, up1, up2):
                    if up2:
                        turned(p, i, k + 2)
                    if up1:
                        hidden(p, i, k + 1)
                    result(p, i, k)

                tiles(dve, tile_step)
                combine(p)


def kernel(**inputs):
    import numpy as np
    import concourse.bacc as bacc
    from concourse.bass_utils import run_bass_kernel_spmd

    a = {k: np.asarray(v) for k, v in inputs.items()}
    w1, w2 = a["L0_ffn_W1"], a["L0_ffn_W2"]
    experts = np.concatenate([
        w1,
        a["L0_ffn_b1"].reshape(E, HC, P).transpose(0, 2, 1),
        w2.reshape(E, HC, P, D).transpose(0, 2, 1, 3).reshape(E, P, HC * D),
        np.broadcast_to(a["L0_ffn_b2"][:, None, :], (E, P, D)),
    ], axis=2)
    by_dim = np.arange(D).reshape(HEADS, HD).T.ravel()
    wqkv = np.stack([a["L0_attn_Wq"].T[:, by_dim], a["L0_attn_Wk"].T[:, by_dim], a["L0_attn_Wv"].T], axis=1)
    bqk = np.stack([a["L0_attn_bq"][by_dim], a["L0_attn_bk"][by_dim]], axis=1)
    bvo = np.stack([a["L0_attn_bv"], a["L0_attn_bo"]])
    attn = {"wqkv": wqkv, "wo": a["L0_attn_Wo"].T, "bqk": bqk, "bvo": bvo}
    arrays = {"x": a["L0_attn_x"].reshape(TOKENS, D), "wr": a["L0_ffn_Wr"], "br": a["L0_ffn_br"], "experts": experts, **attn}
    arrays = {k: np.ascontiguousarray(v) for k, v in arrays.items()}
    nc = bacc.Bacc("TRN2", target_bir_lowering=False, num_devices=1)
    t = {k: nc.dram_tensor("in_" + k, v.shape, F32, kind="ExternalInput").ap() for k, v in arrays.items()}
    out = nc.dram_tensor("out", (TOKENS, D), F32, kind="ExternalOutput").ap()
    build(nc, t["x"], t["wr"], t["br"], t["experts"], t["wqkv"], t["wo"], t["bqk"], t["bvo"], out)
    r = run_bass_kernel_spmd(nc, [{"in_" + k: v for k, v in arrays.items()}], core_ids=[0])
    return r.results[0]["out"].reshape(8, 512, D)
```

```python
from contextlib import ExitStack

import concourse.bass as bass
from concourse import mybir

F32 = mybir.dt.float32
BF16 = mybir.dt.bfloat16
I32 = mybir.dt.int32
ALU = mybir.AluOpType
ACT = mybir.ActivationFunctionType
AX = mybir.AxisListType

P = 128
F32R = mybir.dt.float32r
BANK = 512
TOKENS = 8 * 512
TT = TOKENS // P
NB = 8
S = 512
BT = S // P
HEADS = 16
HD = 8
G = 4
J = HEADS // G
D = 128
E = 8
H = 512
HC = H // P
TOPK = 2
NT = TOPK * TOKENS // P + E - 1
MAXT = TOKENS // P
EPS = 1e-5
B1_AT, B2_AT, W2_AT = H, H + HC, H + HC + D
WROW = W2_AT + HC * D
AHEAD = 4
LAG = 6
HOTS = 4
CHUNKS = 4
CT = TT // CHUNKS
HALVES = 2
HT = TT // HALVES
SEQS = 2


PARTS = 4 * HD
SHIFT = PARTS
DEN = HD

SPARE = {(0, 0): "turn_max", (0, 1): "turn_acc", (0, 2): "q", (0, 3): "k",
         (1, 0): "turn_max", (1, 1): "turn_attn", (1, 2): "turn_acc", (1, 3): "project",
         (2, 0): "turn_max", (2, 1): "turn_acc", (2, 2): "v",
         (3, 0): "turn_max", (3, 1): "turn_acc", (3, 2): "turn_x"}
BEFORE = ("turn_attn", "project")
NEXT = ("q", "k", "v")
STATISTICS = ((1, 1), (1, 3), (2, 1), (2, 3))


def build(nc, x_in, wr_in, br_in, experts, wqkv_in, wo_in, bqk_in, bvo_in, out):
    with ExitStack() as ctx:
        def sb(name, shape, dt=F32):
            return ctx.enter_context(nc.sbuf_tensor(name, shape, dt))

        def sem(name):
            return ctx.enter_context(nc.semaphore(name))

        psum = ctx.enter_context(nc.psum_tensor("psum", [P, 8, BANK], F32))
        xn_rows = nc.dram_tensor("xn_rows", [TOKENS, D], F32).ap()
        y_rows = nc.dram_tensor("y_rows", [TOPK * TOKENS + NT * P, D], F32).ap()

        x = sb("x", [P, TT, D])
        xn = sb("xn", [P, TT, D])
        stats = sb("stats", [P, TT, 6])
        meanvar = sb("meanvar", [P, TT, 2])
        var_eps = sb("var_eps", [P, TT])
        rstd = sb("rstd", [P, TT])
        weight = sb("weight", [P, TOPK, TT])
        rows = sb("rows", [P, SEQS, BT, TOPK, D])
        neg_half = sb("neg_half", [P, TT])
        ident = sb("ident", [P, P])
        wr = sb("wr", [D, E])
        br = sb("br", [P, E])
        before = sb("before", [P, P], BF16)
        ones_bf = sb("ones_bf", [P, P], BF16)
        e_rev = sb("e_rev", [P, TT, E])
        tile_steps = sb("tile_steps", [P, E, MAXT])
        tile_no = sb("tile_no", [P, NT, E])
        restart = sb("restart", [P, E, TT])
        ones_e = sb("ones_e", [P, E])
        lane = sb("lane", [P, P], BF16)
        tile_count = sb("tile_count", [P, NT], BF16)
        partition_1 = sb("partition_1", [P, 1])
        unused_no = sb("unused_no", [P, NT])
        w_all = sb("w_all", [P, E, WROW])
        wqkv = sb("wqkv", [D, 3, D])
        wo = sb("wo", [D, D])
        bqk = sb("bqk", [P, 2])
        bvo = sb("bvo", [P, 2, D])
        qk_rows = nc.dram_tensor("qk_rows", [2, 2, P, S], F32).ap()
        max_rows = nc.dram_tensor("max_rows", [2, J, S], F32).ap()
        qx = sb("qx", [P, G, J, S], F32R)
        kx = sb("kx", [P, G, J, S], F32R)

        with ExitStack() as ffn_only:
            def sb_ffn(name, shape, dt=F32):
                return ffn_only.enter_context(nc.sbuf_tensor(name, shape, dt))

            xnT = sb_ffn("xnT", [P, 2, BANK])
            scoreT = sb_ffn("scoreT", [E, 2, BANK])
            score = sb_ffn("score", [P, TT, E])
            score2 = sb_ffn("score2", [P, TT, E])
            hit = sb_ffn("hit", [P, TT, E])
            pick = [sb_ffn(f"pick{j}", [P, TT, E]) for j in range(TOPK)]
            picked = sb_ffn("picked", [P, TT, E], BF16)
            best = [sb_ffn(f"best{j}", [P, TT]) for j in range(TOPK)]
            key = sb_ffn("key", [P, TT])
            gap = sb_ffn("gap", [P, TT])
            den = sb_ffn("den", [P, TT])
            totals = sb_ffn("totals", [P, E, TT])
            running = sb_ffn("running", [P, E, TT])
            fill = sb_ffn("fill", [P, E, MAXT])
            tiles_e = sb_ffn("tiles_e", [P, E])
            ends = sb_ffn("ends", [P, E])
            base = sb_ffn("base", [P, E])
            where = sb_ffn("where", [P, TT, E])
            where_j = [sb_ffn(f"where_{j}", [P, TT, E]) for j in range(TOPK)]
            slot_f = sb_ffn("slot_f", [P, TOPK, TT])
            slot = sb_ffn("slot", [P, TOPK, TT], I32)
            lane_int = sb_ffn("lane_int", [P, TOPK, TT], I32)
            tile_int = sb_ffn("tile_int", [P, TOPK, TT], I32)
            slot_lane = sb_ffn("slot_lane", [P, TOPK, TT])
            slot_tile = sb_ffn("slot_tile", [P, TOPK, TT])
            past = sb_ffn("past", [P, NT, E])
            expert_f = sb_ffn("expert_f", [P, NT])
            expert = sb_ffn("expert", [P, NT], I32)
            in_lane = sb_ffn("in_lane", [P, HOTS, TOPK, P], BF16)
            in_tile = sb_ffn("in_tile", [P, HOTS, TOPK, NT], BF16)
            tile_row = sb_ffn("tile_row", [P, HOTS, TOPK, 2, NT], BF16)
            row_high = sb_ffn("row_high", [P, NT])
            unused = sb_ffn("unused", [P, NT])
            row_f = sb_ffn("row_f", [P, NT])
            row_of = sb_ffn("row_of", [P, NT], I32)
            token = sb_ffn("token", [P, NT], I32)
            w_up = sb_ffn("w_up", [P, AHEAD, W2_AT])
            xs = sb_ffn("xs", [P, AHEAD, D])
            xsT = sb_ffn("xsT", [P, 2, P])
            hT = sb_ffn("hT", [P, 2, HC, P])
            ys = sb_ffn("ys", [P, AHEAD, D])

        probs = xn[:].rearrange("p t d -> p (t d)").rearrange("p (b j s) -> p b j s", b=2, j=J)
        vx = sb("vx", [P, BT, HEADS, 32])
        v_rows = sb("v_rows", [P, BT, HEADS, HD])
        xb = sb("xb", [P, BT, D])
        xbT = sb("xbT", [P, S])
        q_parts = sb("q_parts", [P, 2, S], F32R)
        k_parts = sb("k_parts", [P, 2, S], F32R)
        neg_max = sb("neg_max", [P, 2, J, BT])
        max_parts = sb("max_parts", [J, 2, S], F32R)
        acc_sb = sb("acc_sb", [P, 2, S])
        recip = sb("recip", [P, BT, J])
        attn = sb("attn", [P, BT, HEADS, HD])
        attnT = sb("attnT", [D, S])

        consts = sem("consts")
        sp_waited = sem("sp_waited")
        pool_waited = sem("pool_waited")
        dve_waited = sem("dve_waited")
        at_consts = sem("at_consts")
        at_loaded = sem("at_loaded")
        centered = sem("centered")
        xb_ready = sem("xb_ready")
        xbT_ps = sem("xbT_ps")
        xbT_sb = sem("xbT_sb")
        qk_ps = sem("qk_ps")
        qk_high = sem("qk_high")
        qk_low = sem("qk_low")
        v_ps = sem("v_ps")
        v_sb = sem("v_sb")
        vx_ready = sem("vx_ready")
        bo_added = sem("bo_added")
        qk_stored = [sem(f"{n}_stored") for n in "qk"]
        qkx_in = [sem(f"qkx_in{g}") for g in range(G)]
        max_stored = sem("max_stored")
        max_in = [sem(f"max_in{g}") for g in range(G)]
        s_ps = sem("s_ps")
        s_max = sem("s_max")
        maxT_ps = sem("maxT_ps")
        max_sb = sem("max_sb")
        st_ps = sem("st_ps")
        exp_sb = sem("exp_sb")
        pv_ps = sem("pv_ps")
        acc_out = sem("acc_out")
        acc_turned = sem("acc_turned")
        recip_ready = sem("recip_ready")
        attn_ready = sem("attn_ready")
        attn_turned = sem("attn_turned")
        attnT_sb = sem("attnT_sb")
        o_ps = sem("o_ps")
        o_sb = sem("o_sb")
        max_high = sem("max_high")
        x_loaded = [sem(f"x_loaded{q}") for q in range(CHUNKS)]
        router_in = sem("router_in")
        experts_in = sem("experts_in")
        xn_out = sem("xn_out")
        dve_step = sem("dve_step")
        pool_step = sem("pool_step")
        var_ready = sem("var_ready")
        rstd_ready = sem("rstd_ready")
        xn_ready = sem("xn_ready")
        xnT_ps = sem("xnT_ps")
        xnT_sb = sem("xnT_sb")
        scoreT_ps = sem("scoreT_ps")
        scoreT_sb = sem("scoreT_sb")
        routed_ps = sem("routed_ps")
        gap_ready = sem("gap_ready")
        gap_exp = sem("gap_exp")
        picked_ready = sem("picked_ready")
        counts_ps = sem("counts_ps")
        slots_ready = sem("slots_ready")
        experts_known = sem("experts_known")
        pool_hot = sem("pool_hot")
        dve_hot = sem("dve_hot")
        rows_hot = sem("rows_hot")
        slot_map_ps = sem("slot_map_ps")
        tokens_ready = sem("tokens_ready")
        w_up_sb = sem("w_up_sb")
        xs_in = [sem(f"xs_in{i}") for i in range(AHEAD)]
        xsT_ps = sem("xsT_ps")
        xsT_sb = sem("xsT_sb")
        h_ps = sem("h_ps")
        h_act = sem("h_act")
        h_dve = sem("h_dve")
        y_ps = sem("y_ps")
        y_sb = sem("y_sb")
        y_out = [sem(f"y_out{i}") for i in range(AHEAD)]
        rows_in = [sem(f"rows_in{i}") for i in range(SEQS)]
        seq_weighted = [sem(f"seq_weighted{j}") for j in range(TOPK)]
        seq_first = sem("seq_first")
        combined = sem("combined")
        seq_stats = sem("seq_stats")
        seq_meanvar = sem("seq_meanvar")
        seq_combined = sem("seq_combined")
        stored = sem("stored")

        ps_st = [psum[:, 2 * i:2 * i + 2, :] for i in range(2)]
        ps_s = [psum[:, 4 + i, :] for i in range(2)]
        ps_first = [psum[:, i, :] for i in range(4)]
        ps_acc = psum[:, 6, :]
        ps_spare = psum[:, 7, :]
        ps_t = [psum[:, 6 + i, :] for i in range(2)]
        ps_slot_map = psum[:, 2, 0:2 * NT].rearrange("p (a n) -> p a n", a=2)
        ps_h = [[psum[:, 2 * i + c // 2, c % 2 * P:(c % 2 + 1) * P] for c in range(HC)] for i in range(2)]
        ps_y = [psum[:, 4 + i, 0:D] for i in range(2)]
        ps_score = [psum[:, 2 + q, 0:HT * E].rearrange("p (t e) -> p t e", e=E) for q in range(HALVES)]
        ps_rank = psum[:, 0, 0:TT * E].rearrange("p (t e) -> p t e", e=E)
        ps_total = psum[:, 1, 0:TT * E].rearrange("p (t e) -> p t e", e=E)

        xn_rows_v = xn_rows.rearrange("(t p) d -> p t d", p=P)
        y_rows_v = y_rows[0:TOPK * TOKENS].rearrange("(j b t p) d -> b p t j d", p=P, j=TOPK, t=BT)
        x_v = x_in.rearrange("(t p) d -> p t d", p=P)
        out_v = out.rearrange("(t p) d -> p t d", p=P)
        PHASES = 2
        QKX = 16 * 5

        def one(i):
            return bass.ds(i, 1)

        def wait(eng, semaphore, count):
            if not isinstance(count, int) or count > 0:
                eng.wait_ge(semaphore, count)

        def wait_alone(eng, semaphore, count, carrier=sp_waited):
            if not isinstance(count, int) or count > 0:
                eng.wait_ge(semaphore, count)
                eng.sem_inc(carrier, 1)

        def sequences(eng, run):
            run(0, True, 2)
            with eng.Fori(1, NB - 2) as b:
                run(b, False, 2)
            run(NB - 2, False, 1)
            run(NB - 1, False, 0)

        def tasks(g, c, first, after):
            what = SPARE.get((g, c))
            if after == 0 and (what in NEXT or (what == "turn_max" and g == G - 1)):
                return None
            if after < 2 and what == "turn_x":
                return None
            if first and (what in BEFORE or (what == "turn_acc" and g == 0)):
                return None
            return what

        def done(n):
            return n + 3

        def tile_of(p, i, k):
            return p * NT + 4 * i + k, (p * NT + k) % 2

        def uses_of(p, k):
            return p * ((NT + AHEAD - 1 - k) // AHEAD)

        def tiles(eng, step):
            for k in range(4):
                step(0, k, True, True)
            with eng.Fori(1, (NT - 2) // 4) as i:
                for k in range(4):
                    step(i, k, True, True)
            for n in range((NT - 2) // 4 * 4, NT):
                step(n // 4, n % 4, n + 1 < NT, n + 2 < NT)

        block = ctx.enter_context(nc.Block())

        @block.gpsimd
        def _(pool):
            n = [0]

            def step(ins):
                ins.then_inc(pool_step, 1)
                n[0] += 1
                pool.wait_ge(pool_step, n[0])

            step(nc.gpsimd.memset(ident[:], 0.0))
            step(nc.gpsimd.memset(before[:], 1.0))
            step(nc.gpsimd.affine_select(out=ident[:], in_=ident[:], compare_op=ALU.not_equal, fill=1.0,
                                         base=0, pattern=[[-1, P]], channel_multiplier=1))
            step(nc.gpsimd.affine_select(out=before[:], in_=before[:], compare_op=ALU.is_gt, fill=0.0,
                                         base=0, pattern=[[1, P]], channel_multiplier=-1))
            step(nc.gpsimd.memset(ones_bf[:], 1.0))
            step(nc.gpsimd.memset(neg_half[:], -0.5))
            step(nc.gpsimd.memset(ones_e[:], 1.0))
            step(nc.gpsimd.memset(restart[:], 1.0))
            step(nc.gpsimd.memset(restart[:, :, 0:1], 0.0))
            step(nc.gpsimd.iota(e_rev[:], [[0, TT], [-1, E]], base=E, channel_multiplier=0,
                                allow_small_or_imprecise_dtypes=True))
            step(nc.gpsimd.iota(tile_steps[:], [[0, E], [P, MAXT]], base=0, channel_multiplier=0,
                                allow_small_or_imprecise_dtypes=True))
            nc.gpsimd.iota(tile_no[:], [[1, NT], [0, E]], base=0, channel_multiplier=0,
                           allow_small_or_imprecise_dtypes=True).then_inc(pool_step, 1)
            n[0] += 1
            pool.wait_ge(pool_step, n[0])
            step(nc.gpsimd.iota(lane[:], [[1, P]], base=0, channel_multiplier=0, allow_small_or_imprecise_dtypes=True))
            step(nc.gpsimd.iota(tile_count[:], [[1, NT]], base=0, channel_multiplier=0,
                                allow_small_or_imprecise_dtypes=True))
            step(nc.gpsimd.iota(unused_no[:], [[P, NT]], base=1 + TOPK * TOKENS, channel_multiplier=1,
                                allow_small_or_imprecise_dtypes=True))
            nc.gpsimd.iota(partition_1[:], [[0, 1]], base=1, channel_multiplier=1,
                           allow_small_or_imprecise_dtypes=True).then_inc(consts, 1)
            def attention_consts():
                step(nc.gpsimd.memset(qx[:].bitcast(F32), 0.0))
                step(nc.gpsimd.memset(kx[:].bitcast(F32), 0.0))
                nc.gpsimd.memset(kx[SHIFT:SHIFT + 2].bitcast(F32), 1.0).then_inc(at_consts, 1)
                pool.wait_ge(at_consts, 1)

            def expand_v(b, g):
                wait_alone(pool, pv_ps, 16 * b - 16 + 4 * g + 4, pool_waited)
                wait_alone(pool, v_sb, b + 1, pool_waited)
                nc.gpsimd.tensor_copy(vx[:, :, J * g:J * g + J, 0:HD], v_rows[:, :, J * g:J * g + J, :]).then_inc(vx_ready, 1)

            def add_bo(b):
                wait_alone(pool, xb_ready, b + 1, pool_waited)
                nc.gpsimd.tensor_tensor(x[:, bass.ds(4 * b, BT), :], x[:, bass.ds(4 * b, BT), :],
                                        bvo[:, 1:2, :].to_broadcast([P, BT, D]), ALU.add).then_inc(bo_added, 1)

            def combine(b):
                wait_alone(pool, rows_in[0], 16 * TOPK * (b + 1), pool_waited)
                for j in range(TOPK):
                    part = rows[:, 0, :, j, :]
                    nc.gpsimd.tensor_tensor(part, part, weight[:, j, bass.ds(BT * b, BT)].unsqueeze(2).to_broadcast([P, BT, D]),
                                            ALU.mult).then_inc(seq_weighted[j], 1)
                seq = x[:, bass.ds(BT * b, BT), :]
                wait_alone(pool, seq_weighted[0], b + 1, pool_waited)
                nc.gpsimd.tensor_tensor(seq, seq, rows[:, 0, :, 0, :], ALU.add).then_inc(seq_first, 1)
                wait_alone(pool, seq_weighted[1], b + 1, pool_waited)
                wait_alone(pool, seq_first, b + 1, pool_waited)
                nc.gpsimd.tensor_tensor(seq, seq, rows[:, 0, :, 1, :], ALU.add).then_inc(seq_combined, 1)
                wait_alone(pool, seq_combined, b + 1, pool_waited)

            def norm(b):
                pool.wait_ge(var_ready, CHUNKS + b + 1)
                nc.gpsimd.tensor_tensor(rstd[:, 0:BT], var_eps[:, 0:BT], neg_half[:, 0:BT], ALU.pow).then_inc(rstd_ready, 1)
                wait_alone(pool, rstd_ready, CHUNKS + b + 1, pool_waited)
                wait_alone(pool, xbT_ps, b, pool_waited)
                nc.gpsimd.tensor_tensor(xb[:], x[:, bass.ds(BT * b, BT), :], meanvar[:, 0:BT, 0:1].to_broadcast([P, BT, D]),
                                        ALU.subtract).then_inc(centered, 1)
                pool.wait_ge(centered, b + 1)
                nc.gpsimd.tensor_tensor(xb[:], xb[:], rstd[:, 0:BT].unsqueeze(2).to_broadcast([P, BT, D]), ALU.mult).then_inc(xb_ready, 1)

            def attention():
                combine(0)
                norm(0)
                step(nc.gpsimd.memset(vx[:], 0.0))
                step(nc.gpsimd.memset(vx[:, :, :, DEN:DEN + 1], 1.0))
                add_bo(0)
                combine(1)
                norm(1)
                for g in range(G):
                    expand_v(0, g)

                def run(b, first, after):
                    if after:
                        add_bo(b + 1)
                    if not first:
                        expand_v(b, G - 1)
                    if after == 2:
                        combine(b + 2)
                    if after:
                        expand_v(b + 1, 0)
                        expand_v(b + 1, 1)
                    if after == 2:
                        norm(b + 2)
                    if after:
                        expand_v(b + 1, 2)

                sequences(pool, run)

            for p in range(PHASES):
                if p == 1:
                    pool.wait_ge(at_loaded, 16 * 4)
                    attention()
                for q in range(CHUNKS):
                    part = slice(CT * q, CT * q + CT)
                    pool.wait_ge(var_ready, p * (CHUNKS + NB) + q + 1)
                    nc.gpsimd.tensor_tensor(rstd[:, part], var_eps[:, part], neg_half[:, part], ALU.pow).then_inc(rstd_ready, 1)
                if p == 0:
                    attention_consts()
                pool.wait_ge(slots_ready, p + 1)
                for t in range(TT):
                    pool.wait_ge(slot_map_ps, p * TT + t + 1)
                    nc.gpsimd.tensor_scalar(in_lane[:, t % HOTS, 0, :], lane[:], slot_lane[:, 0, t:t + 1], None,
                                            ALU.is_equal).then_inc(pool_hot, 1)
                pool.wait_ge(xn_out, 16 * (TT // 4) * (p + 1))
                pool.wait_ge(tokens_ready, p + 1)
                for t in range(NT + LAG):
                    if t < NT:
                        if t >= AHEAD:
                            pool.wait_ge(xsT_ps, done(p * NT + t - AHEAD))
                        elif p and t == 0:
                            pool.wait_ge(xsT_ps, done(p * NT - 1))
                        nc.gpsimd.indirect_dma_start(
                            xs[:, t % AHEAD, :], None, xn_rows,
                            bass.IndirectOffsetOnAxis(ap=token[:, t:t + 1], axis=0)).then_inc(xs_in[t % AHEAD], 16)
                    m = t - LAG
                    if m >= 0:
                        pool.wait_ge(y_sb, done(p * NT + m))
                        nc.gpsimd.indirect_dma_start(
                            y_rows, bass.IndirectOffsetOnAxis(ap=row_of[:, m:m + 1], axis=0),
                            ys[:, m % AHEAD, :], None).then_inc(y_out[m % AHEAD], 16)

        @block.sync
        def _(sp):
            for q in range(CHUNKS):
                sp.dma_start(x[:, CT * q:CT * q + CT, :], x_v[:, CT * q:CT * q + CT, :]).then_inc(x_loaded[q], 16)
            sp.dma_start(wr[:], wr_in).then_inc(router_in, 16)
            sp.dma_start(br[:], br_in.partition_broadcast(P)).then_inc(router_in, 16)
            for e in range(E):
                sp.dma_start(w_all[:, e, :], experts[e]).then_inc(experts_in, 16)
            sp.dma_start(wqkv[:], wqkv_in).then_inc(at_loaded, 16)
            sp.dma_start(bqk[:], bqk_in).then_inc(at_loaded, 16)
            sp.dma_start(bvo[:], bvo_in.partition_broadcast(P)).then_inc(at_loaded, 16)
            sp.dma_start(wo[:], wo_in).then_inc(at_loaded, 16)

            def store_qk(b, which):
                wait_alone(sp, qk_low, 2 * b + which + 1)
                for g in range(G):
                    wait_alone(sp, qkx_in[g], QKX * b)
                parts = (q_parts, k_parts)[which]
                sp.dma_start(qk_rows[which].rearrange("h p n -> p h n"), parts[:].bitcast(F32)).then_inc(qk_stored[which], 16)

            def expand_qk(b, g):
                for s in qk_stored:
                    wait_alone(sp, s, 16 * (b + 1))
                wait_alone(sp, st_ps, 32 * b - 32 + 8 * g + 8)
                q_of, k_of = (qk_rows[i].rearrange("h (d g j) n -> g h d (j n)", d=HD, g=G)[g] for i in range(2))
                for h in range(2):
                    sp.dma_start(qx[2 * HD * h:2 * HD * (h + 1), g, :, :].rearrange("p j n -> p (j n)").bitcast(F32),
                                 q_of[h].unsqueeze(0).to_broadcast([2, HD, J * S])).then_inc(qkx_in[g], 16)
                for r in range(2):
                    sp.dma_start(kx[2 * HD * r:2 * HD * (r + 1), g, :, :].rearrange("p j n -> p (j n)").bitcast(F32), k_of).then_inc(qkx_in[g], 16)
                sp.dma_start(qx[SHIFT:SHIFT + 2, g, :, :].rearrange("p j n -> p (j n)").bitcast(F32),
                             qx[SHIFT + 2:SHIFT + 4, g, :, :].rearrange("p j n -> p (j n)").bitcast(F32)).then_inc(qkx_in[g], 16)

            def place_max(b, g):
                u = 4 * b + g
                wait_alone(sp, max_sb, u + 1)
                if g:
                    wait_alone(sp, max_in[g - 1], 16 * (b + 1))
                else:
                    wait_alone(sp, max_in[G - 1], 16 * b)
                sp.dma_start(max_rows.rearrange("h j n -> j h n"), max_parts[:].bitcast(F32)).then_inc(max_stored, 16)
                wait_alone(sp, max_stored, 16 * (u + 1))
                sp.dma_start(qx[SHIFT:SHIFT + 2, g, :, :].rearrange("p j n -> p (j n)").bitcast(F32),
                             max_rows.rearrange("h j n -> h (j n)")).then_inc(max_in[g], 16)

            def scattered(p):
                for k in range(AHEAD):
                    sp.wait_ge(y_out[k], 16 * uses_of(p + 1, k))

            def load_results(b, at=0):
                for j in range(TOPK):
                    sp.dma_start(rows[:, at, :, j, :], y_rows_v[one(b), :, :, j, :].rearrange("b p t d -> p (b t) d")).then_inc(rows_in[at], 16)

            def attention():
                scattered(0)
                load_results(0)
                wait_alone(sp, seq_combined, 1)
                load_results(1)
                store_qk(0, 0)
                store_qk(0, 1)
                for g in range(G - 1):
                    expand_qk(0, g)
                place_max(0, 0)

                def run(b, first, after):
                    expand_qk(b, G - 1)
                    if after == 2:
                        wait_alone(sp, seq_combined, b + 2)
                        load_results(b + 2)
                    place_max(b, 1)
                    if after:
                        store_qk(b + 1, 0)
                        store_qk(b + 1, 1)
                        expand_qk(b + 1, 0)
                    place_max(b, 2)
                    if after:
                        expand_qk(b + 1, 1)
                    place_max(b, 3)
                    if after:
                        expand_qk(b + 1, 2)
                        place_max(b + 1, 0)

                sequences(sp, run)

            for p in range(PHASES):
                if p == 1:
                    sp.wait_ge(at_consts, 1)
                    attention()
                for q in range(TT // 4):
                    sp.wait_ge(xn_ready, p * (TT // 4) + q + 1)
                    sp.dma_start(xn_rows_v[:, 4 * q:4 * q + 4, :], xn[:, 4 * q:4 * q + 4, :]).then_inc(xn_out, 16)
            scattered(1)
            for b in range(NB + SEQS):
                if b < NB:
                    wait(sp, combined, BT * (b - SEQS + 1))
                    load_results(b, b % SEQS)
                if b >= SEQS:
                    q = b - SEQS
                    sp.wait_ge(combined, BT * (q + 1))
                    sp.dma_start(out_v[:, BT * q:BT * q + BT, :], x[:, BT * q:BT * q + BT, :]).then_inc(stored, 16)
            sp.wait_ge(stored, 16 * NB)

        @block.scalar
        def _(act):
            def front(p):
                first = p * (TT // 4)
                for q in range(TT // 4 + 1):
                    g = first + q
                    if q < TT // 4:
                        act.wait_ge(xnT_ps, g + 1)
                        act.wait_ge(scoreT_ps, done(g - 2))
                        nc.scalar.activation(xnT[:, q % 2, :], ps_t[q % 2], ACT.Copy).then_inc(xnT_sb, 1)
                    if q:
                        act.wait_ge(scoreT_ps, done(g - 1))
                        act.wait_ge(routed_ps, done(g - 3))
                        nc.scalar.activation(scoreT[:, (q - 1) % 2, :], psum[0:E, (q - 1) % 2, :], ACT.Copy).then_inc(scoreT_sb, 1)

            def fetch(p, i, k):
                n, _ = tile_of(p, i, k)
                e = act.value_load(expert[0:1, one(4 * i + k)], min_val=0, max_val=E - 1)
                wait(act, y_sb, done(n - AHEAD))
                nc.scalar.activation(w_up[:, k % AHEAD, :], w_all[:, one(e), 0:W2_AT], ACT.Copy).then_inc(w_up_sb, 1)

            def hidden(p, i, k):
                n, b = tile_of(p, i, k)
                act.wait_ge(h_ps, done(n))
                act.wait_ge(w_up_sb, done(n))
                act.wait_ge(y_ps, done(n - 2))
                for c in range(HC // 2):
                    last = nc.scalar.activation(hT[:, b, c, :], ps_h[b][c], ACT.Relu,
                                                bias=w_up[:, k % AHEAD, B1_AT + c:B1_AT + c + 1])
                last.then_inc(h_act, 1)

            def turn_x_out(b):
                act.wait_ge(xbT_ps, b + 1)
                wait(act, v_ps, b)
                nc.scalar.activation(xbT[:], ps_spare, ACT.Copy).then_inc(xbT_sb, 1)

            def high(b, which):
                act.wait_ge(qk_ps, 2 * b + which + 1)
                wait(act, qk_stored[which], 16 * b)
                parts = (q_parts, k_parts)[which]
                nc.scalar.activation(parts[:, 0, :], ps_spare, ACT.Identity, bias=bqk[:, which:which + 1]).then_inc(qk_high, 1)

            def turn_attn_out(b):
                act.wait_ge(attn_turned, b + 1)
                wait(act, o_ps, b)
                nc.scalar.activation(attnT[:], ps_spare, ACT.Copy).then_inc(attnT_sb, 1)

            def max_high_part(b, g):
                u = 4 * b + g
                act.wait_ge(maxT_ps, u + 1)
                wait(act, max_stored, 16 * u)
                nc.scalar.activation(max_parts[:, 0, :], ps_spare[0:J, :], ACT.Copy).then_inc(max_high, 1)

            def exps(b, g, c, half):
                step = 16 * b + 4 * g + c
                act.wait_ge(st_ps, 2 * step + half + 1)
                wait(act, pv_ps, step - 1)
                nc.scalar.activation(probs[:, c % 2, 2 * half:2 * half + 2, :], ps_st[half], ACT.Exp,
                                     scale=HD ** -0.5).then_inc(exp_sb, 1)

            def acc_done(b, g):
                u = 4 * b + g
                act.wait_ge(pv_ps, 4 * u + 4)
                wait(act, acc_turned, u - 1)
                nc.scalar.activation(acc_sb[:, g % 2, :], ps_acc, ACT.Copy).then_inc(acc_out, 1)

            def attention():
                turn_x_out(0)
                high(0, 0)
                high(0, 1)
                turn_x_out(1)
                max_high_part(0, 0)

                def run(b, first, after):
                    for g in range(G):
                        for c in range(BT):
                            what = tasks(g, c - 1, first, after) if c else tasks(g - 1, BT - 1, first, after)
                            if what == "turn_max":
                                at = (4 * g + c - 1) // 4 + 1
                                max_high_part(b + at // G, at % G)
                            elif what == "turn_x":
                                turn_x_out(b + 2)
                            elif what == "q":
                                high(b + 1, 0)
                            elif what == "k":
                                high(b + 1, 1)
                            elif what == "turn_attn":
                                turn_attn_out(b - 1)
                            exps(b, g, c, 0)
                            exps(b, g, c, 1)
                            if c == 0 and not (first and g == 0):
                                acc_done(b - (g == 0), (g - 1) % G)

                sequences(act, run)
                acc_done(NB - 1, G - 1)
                turn_attn_out(NB - 1)

            for s in (xnT_sb, h_act, w_up_sb):
                act.sem_inc(s, 2)
            for p in range(PHASES):
                if p == 1:
                    attention()
                front(p)
                act.wait_ge(slots_ready, p + 1)
                for t in range(TT):
                    act.wait_ge(dve_hot, p * TT + t + 1)
                    act.wait_ge(slot_map_ps, p * TT + t + 1)
                    at = t % HOTS
                    nc.scalar.activation(tile_row[:, at, :, 0, :], in_tile[:, at, :, :], ACT.Copy, scale=partition_1[:])
                    for j in range(TOPK):
                        last = nc.scalar.activation(tile_row[:, at, j, 1, :], in_tile[:, at, j, :], ACT.Copy,
                                                    scale=float(TT * j + t))
                    last.then_inc(rows_hot, 1)
                if p == 0:
                    act.wait_ge(experts_in, 16 * E)
                act.wait_ge(gap_ready, p + 1)
                nc.scalar.activation(gap[:], gap[:], ACT.Exp).then_inc(gap_exp, 1)
                act.wait_ge(experts_known, p + 1)
                fetch(p, 0, 0)
                fetch(p, 0, 1)
                hidden(p, 0, 0)

                def step(i, k, up1, up2):
                    if up2:
                        fetch(p, i, k + 2)
                    if up1:
                        hidden(p, i, k + 1)

                tiles(act, step)

        @block.tensor
        def _(pe):
            for s in (scoreT_ps, routed_ps, xsT_ps, h_ps, y_ps):
                pe.sem_inc(s, 2)
            pe.sem_inc(slot_map_ps, HOTS)

            def front(p):
                first = p * (TT // 4)
                for q in range(TT // 4 + 2):
                    if q < TT // 4:
                        pe.wait_ge(xn_ready, first + q + 1)
                        pe.wait_ge(xnT_sb, done(first + q - 2))
                        for j in range(4):
                            mm = nc.tensor.transpose(ps_t[q % 2][:, j * P:(j + 1) * P], xn[:, 4 * q + j, :], ident[:])
                        mm.then_inc(xnT_ps, 1)
                    if 1 <= q <= TT // 4:
                        g = first + q - 1
                        pe.wait_ge(xnT_sb, done(g))
                        wait(pe, scoreT_sb, g - 1)
                        nc.tensor.matmul(psum[0:E, (q - 1) % 2, :], wr[:], xnT[:, (q - 1) % 2, :], start=True, stop=True).then_inc(scoreT_ps, 1)
                    if q >= 2:
                        at = 4 * (q - 2)
                        pe.wait_ge(scoreT_sb, first + q - 1)
                        for j in range(4):
                            mm = nc.tensor.transpose(ps_score[at // HT][:, at % HT + j, :], scoreT[:, q % 2, j * P:(j + 1) * P], ident[0:E, 0:E])
                        mm.then_inc(routed_ps, 1)
                pe.wait_ge(picked_ready, HALVES * (p + 1))
                rhs = picked[:].rearrange("p t e -> p (t e)")
                nc.tensor.matmul(psum[:, 0, 0:TT * E], before[:], rhs, start=True, stop=True)
                nc.tensor.matmul(psum[:, 1, 0:TT * E], ones_bf[:], rhs, start=True, stop=True).then_inc(counts_ps, 1)
                for t in range(TT):
                    pe.wait_ge(pool_hot, p * TT + t + 1)
                    pe.wait_ge(rows_hot, p * TT + t + 1)
                    for j in range(TOPK):
                        mm = nc.tensor.matmul(psum[:, 2, 0:2 * NT], in_lane[:, t % HOTS, j, :],
                                              tile_row[:, t % HOTS, j, :, :].rearrange("p a n -> p (a n)"),
                                              start=(t == 0 and j == 0), stop=(t == TT - 1 and j == TOPK - 1))
                    mm.then_inc(slot_map_ps, 1)

            def turn(p, i, k):
                n, b = tile_of(p, i, k)
                at = k % AHEAD
                pe.wait_ge(xs_in[at], 16 * (uses_of(p, at) + i + k // AHEAD + 1))
                pe.wait_ge(xsT_sb, done(n - 2))
                nc.tensor.transpose(ps_t[b][:, 0:P], xs[:, at, :], ident[:]).then_inc(xsT_ps, 1)

            def up(p, i, k):
                n, b = tile_of(p, i, k)
                pe.wait_ge(xsT_sb, done(n))
                pe.wait_ge(w_up_sb, done(n))
                pe.wait_ge(h_act, done(n - 2))
                pe.wait_ge(h_dve, done(n - 2))
                for c in range(HC):
                    mm = nc.tensor.matmul(ps_h[b][c], w_up[:, k % AHEAD, c * P:(c + 1) * P], xsT[:, b, :],
                                          start=True, stop=True)
                mm.then_inc(h_ps, 1)

            def down(p, i, k):
                n, b = tile_of(p, i, k)
                e = pe.value_load(expert[0:1, one(4 * i + k)], min_val=0, max_val=E - 1)
                pe.wait_ge(h_act, done(n))
                pe.wait_ge(h_dve, done(n))
                pe.wait_ge(y_sb, done(n - 2))
                for c in range(HC):
                    mm = nc.tensor.matmul(ps_y[b], hT[:, b, c, :],
                                          w_all[:, one(e), W2_AT + c * D:W2_AT + (c + 1) * D].rearrange("p e n -> p (e n)"),
                                          start=(c == 0), stop=(c == HC - 1))
                mm.then_inc(y_ps, 1)

            def turn_x(b):
                pe.wait_ge(xb_ready, b + 1)
                for j in range(BT):
                    mm = nc.tensor.transpose(ps_spare[:, j * P:(j + 1) * P], xb[:, j, :], ident[:])
                mm.then_inc(xbT_ps, 1)

            def project_qk(b, which):
                pe.wait_ge(xbT_sb, b + 1)
                nc.tensor.matmul(ps_spare, wqkv[:, which, :], xbT[:], start=True, stop=True).then_inc(qk_ps, 1)

            def project_v(b):
                for j in range(BT):
                    mm = nc.tensor.matmul(ps_spare[:, j * P:(j + 1) * P], xbT[:, j * P:(j + 1) * P], wqkv[:, 2, :],
                                          start=True, stop=True)
                mm.then_inc(v_ps, 1)

            def turn_attn(b):
                pe.wait_ge(attn_ready, 4 * b + 4)
                for c in range(BT):
                    mm = nc.tensor.transpose(ps_spare[:, c * P:(c + 1) * P], attn[:, c, :, :].rearrange("p h d -> p (h d)"), ident[:])
                mm.then_inc(attn_turned, 1)

            def project_out(b):
                pe.wait_ge(attnT_sb, b + 1)
                for c in range(BT):
                    mm = nc.tensor.matmul(ps_spare[:, c * P:(c + 1) * P], attnT[:, c * P:(c + 1) * P], wo[:],
                                          start=True, stop=True)
                mm.then_inc(o_ps, 1)

            def turn_max(b, g):
                pe.wait_ge(s_max, 16 * (4 * b + g) + 16)
                for c in range(BT):
                    mm = nc.tensor.transpose(ps_spare[0:J, c * P:(c + 1) * P], neg_max[:, g % 2, :, c], ident[:])
                mm.then_inc(maxT_ps, 1)

            def turn_acc(b, g):
                pe.wait_ge(acc_out, 4 * b + g + 1)
                for c in range(BT):
                    mm = nc.tensor.transpose(ps_spare[:, c * P:(c + 1) * P], acc_sb[:, g % 2, c * P:(c + 1) * P], ident[:])
                mm.then_inc(acc_turned, 1)

            def scores(b, g, j, c, banks=ps_s):
                if j == 0 and c == 0:
                    pe.wait_ge(qkx_in[g], QKX * (b + 1))
                block = 16 * (4 * b + g) + 4 * j + c
                wait(pe, s_max, block - len(banks) + 1)
                nc.tensor.matmul(banks[c % len(banks)], qx[:, g, j, c * P:(c + 1) * P], kx[:, g, j, :],
                                 start=True, stop=True).then_inc(s_ps, 1)

            def shifted(b, g, c, half):
                if c == 0 and half == 0:
                    pe.wait_ge(max_in[g], 16 * (b + 1))
                wait(pe, exp_sb, 2 * (16 * b + 4 * g + c) + half - 1)
                for i in range(2):
                    j = 2 * half + i
                    mm = nc.tensor.matmul(ps_st[half][:, i, :], kx[:, g, j, c * P:(c + 1) * P], qx[:, g, j, :],
                                          start=True, stop=True)
                mm.then_inc(st_ps, 1)

            def values(b, g, c):
                u = 4 * b + g
                pe.wait_ge(exp_sb, 2 * (4 * u + c) + 2)
                if c == 0:
                    pe.wait_ge(vx_ready, u + 1)
                    wait(pe, acc_out, u)
                for j in range(J):
                    mm = nc.tensor.matmul(ps_acc[32 * j:32 * j + 32, :], vx[:, c, J * g + j, :], probs[:, c % 2, j, :],
                                          start=(c == 0), stop=(c == BT - 1))
                mm.then_inc(pv_ps, 1)

            def attention():
                pe.wait_ge(at_loaded, 16 * 4)
                pe.wait_ge(at_consts, 1)
                turn_x(0)
                project_qk(0, 0)
                pe.wait_ge(qk_low, 1)
                project_qk(0, 1)
                pe.wait_ge(qk_low, 2)
                project_v(0)
                pe.wait_ge(v_sb, 1)
                turn_x(1)
                for u in range(2):
                    for j in range(J):
                        for c in range(BT):
                            scores(0, u, j, c, ps_first)
                    if u == 0:
                        pe.wait_ge(xbT_sb, 2)
                        turn_max(0, 0)
                pe.wait_ge(s_max, 2 * J * BT)

                def run(b, first, after):
                    for g in range(G):
                        ahead = not (after == 0 and g >= 2)
                        for c in range(BT):
                            for half in range(2):
                                shifted(b, g, c, half)
                            for i in range(BT):
                                if i == 3:
                                    spare_task(b, g, c, first, after)
                                if ahead:
                                    scores(b + (g + 2) // G, (g + 2) % G, c, i)
                                if i == 1:
                                    if c:
                                        values(b, g, c - 1)
                                    elif not (first and g == 0):
                                        values(b - (g == 0), (g - 1) % G, BT - 1)

                sequences(pe, run)
                values(NB - 1, G - 1, BT - 1)
                pe.wait_ge(attn_ready, 4 * NB - 1)
                turn_acc(NB - 1, G - 1)
                turn_attn(NB - 1)
                project_out(NB - 1)

            def spare_task(b, g, c, first, after):
                what = tasks(g, c, first, after)
                before = None
                at = 4 * g + c - 1
                while what and before is None and at >= 0:
                    before = tasks(at // 4, at % 4, first, after)
                    at -= 1
                if before is None and what:
                    if first:
                        pe.wait_ge(max_sb, 1)
                    elif after:
                        pe.wait_ge(xbT_sb, b + 2)
                    else:
                        pe.wait_ge(attn_ready, 4 * b - 1)
                    bg = 0
                elif what:
                    bg = (at + 1) // 4
                if before == "turn_max":
                    pe.wait_ge(max_sb, 4 * b + bg + 2)
                elif before == "turn_acc":
                    pe.wait_ge(attn_ready, 4 * b + bg)
                elif before == "turn_attn":
                    pe.wait_ge(attnT_sb, b)
                elif before == "turn_x":
                    pe.wait_ge(xbT_sb, b + 3)
                elif before == "q":
                    pe.wait_ge(qk_low, 2 * b + 3)
                elif before == "k":
                    pe.wait_ge(qk_low, 2 * b + 4)
                elif before == "project":
                    pe.wait_ge(o_sb, b)
                elif before == "v":
                    pe.wait_ge(v_sb, b + 2)
                if what == "turn_max":
                    turn_max(b + (g + 1) // G, (g + 1) % G)
                elif what == "turn_acc":
                    turn_acc(b - (g == 0), (g - 1) % G)
                elif what == "turn_x":
                    turn_x(b + 2)
                elif what == "q":
                    project_qk(b + 1, 0)
                elif what == "k":
                    project_qk(b + 1, 1)
                elif what == "v":
                    project_v(b + 1)
                elif what == "turn_attn":
                    turn_attn(b - 1)
                elif what == "project":
                    project_out(b - 1)

            pe.wait_ge(consts, 1)
            pe.wait_ge(router_in, 32)
            for p in range(PHASES):
                if p == 1:
                    attention()
                front(p)
                pe.wait_ge(experts_known, p + 1)
                if p == 0:
                    pe.wait_ge(experts_in, 16 * E)
                turn(p, 0, 0)
                turn(p, 0, 1)
                up(p, 0, 0)

                def step(i, k, up1, up2):
                    if up2:
                        turn(p, i, k + 2)
                    if up1:
                        up(p, i, k + 1)
                    down(p, i, k)

                tiles(pe, step)

        @block.vector
        def _(dve):
            n = [0]

            def step(ins):
                ins.then_inc(dve_step, 1)
                n[0] += 1
                dve.wait_ge(dve_step, n[0])

            for s in (h_dve, y_sb, xsT_sb):
                dve.sem_inc(s, 2)
            dve.wait_ge(consts, 1)

            def statistics(q):
                chunk = range(CT * q, CT * q + CT)
                for t in chunk:
                    last = nc.vector.bn_stats(stats[:, t, :], x[:, t, :])
                step(last)
                for t in chunk:
                    last = nc.vector.bn_aggr(meanvar[:, t, :], stats[:, t, :])
                step(last)
                part = slice(CT * q, CT * q + CT)
                nc.vector.tensor_scalar(var_eps[:, part], meanvar[:, part, 1], EPS, None, ALU.add).then_inc(var_ready, 1)

            def front(p):
                for q in range(CHUNKS + 1):
                    if p == 0 and q < CHUNKS:
                        dve.wait_ge(x_loaded[q], 16)
                        statistics(q)
                    elif q == CHUNKS - 1:
                        statistics(q)
                    if q:
                        dve.wait_ge(rstd_ready, p * (CHUNKS + NB) + q)
                        for t in range(CT * (q - 1), CT * q):
                            last = nc.vector.tensor_scalar(xn[:, t, :], x[:, t, :], meanvar[:, t, 0:1], rstd[:, t:t + 1],
                                                           ALU.subtract, ALU.mult)
                            if t % 4 == 3:
                                last.then_inc(xn_ready, 1)

            def route(p):
                def over_e(ap):
                    return ap.unsqueeze(2).to_broadcast([P, HT, E])

                if p == 0:
                    dve.wait_ge(router_in, 32)
                for q in range(HALVES):
                    part = slice(HT * q, HT * q + HT)
                    dve.wait_ge(routed_ps, done(p * (TT // 4) + (q + 1) * (HT // 4) - 1))
                    step(nc.vector.tensor_tensor(score[:, part], ps_score[q], br[:].unsqueeze(1).to_broadcast([P, HT, E]), ALU.add))
                    for j in range(TOPK):
                        s = (score if j == 0 else score2)[:, part]
                        step(nc.vector.tensor_reduce(best[j][:, part], s, AX.X, ALU.max))
                        step(nc.vector.tensor_tensor(hit[:, part], s, over_e(best[j][:, part]), ALU.is_equal))
                        step(nc.vector.tensor_tensor(hit[:, part], hit[:, part], e_rev[:, part], ALU.mult))
                        step(nc.vector.tensor_reduce(key[:, part], hit[:, part], AX.X, ALU.max))
                        step(nc.vector.tensor_tensor(pick[j][:, part], e_rev[:, part], over_e(key[:, part]), ALU.is_equal))
                        if j == 0:
                            step(nc.vector.scalar_tensor_tensor(score2[:, part], pick[0][:, part], -3e38, score[:, part], ALU.mult, ALU.add))
                    nc.vector.tensor_tensor(picked[:, part], pick[0][:, part], pick[1][:, part], ALU.add).then_inc(picked_ready, 1)
                dve.wait_ge(counts_ps, p + 1)
                step(nc.vector.tensor_copy(totals[:], ps_total.rearrange("p t e -> p e t")))
                step(nc.vector.tensor_tensor_scan(running[:].rearrange("p e t -> p (e t)"), restart[:].rearrange("p e t -> p (e t)"),
                                                  totals[:].rearrange("p e t -> p (e t)"), 0.0, ALU.mult, ALU.add))
                step(nc.vector.tensor_tensor(fill[:], running[:, :, TT - 1:TT].to_broadcast([P, E, MAXT]), tile_steps[:], ALU.is_gt))
                nc.vector.tensor_reduce(tiles_e[:], fill[:], AX.X, ALU.add)
                step(nc.vector.tensor_tensor(running[:], running[:], totals[:], ALU.subtract))
                nc.vector.tensor_tensor_scan(ends[:], ones_e[:], tiles_e[:], 0.0, ALU.mult, ALU.add)
                step(nc.vector.tensor_tensor(where[:], ps_rank, running[:].rearrange("p e t -> p t e"), ALU.add))
                step(nc.vector.tensor_tensor(base[:], ends[:], tiles_e[:], ALU.subtract))
                step(nc.vector.scalar_tensor_tensor(where[:], base[:].unsqueeze(1).to_broadcast([P, TT, E]), float(P), where[:],
                                                    ALU.mult, ALU.add))
                for j in range(TOPK):
                    last = nc.vector.tensor_tensor(where_j[j][:], where[:], pick[j][:], ALU.mult)
                step(last)
                for j in range(TOPK):
                    last = nc.vector.tensor_reduce(slot_f[:, j, :], where_j[j][:], AX.X, ALU.add)
                step(last)
                step(nc.vector.tensor_copy(slot[:], slot_f[:]))
                nc.vector.tensor_scalar(lane_int[:], slot[:], P - 1, None, ALU.bitwise_and)
                step(nc.vector.tensor_scalar(tile_int[:], slot[:], P.bit_length() - 1, None, ALU.logical_shift_right))
                nc.vector.tensor_copy(slot_lane[:], lane_int[:])
                nc.vector.tensor_copy(slot_tile[:], tile_int[:]).then_inc(slots_ready, 1)

            def mix(p):
                nc.vector.tensor_tensor(gap[:], best[1][:], best[0][:], ALU.subtract).then_inc(gap_ready, 1)
                dve.wait_ge(gap_exp, p + 1)
                step(nc.vector.tensor_scalar(den[:], gap[:], 1.0, None, ALU.add))
                step(nc.vector.reciprocal(den[:], den[:]))
                step(nc.vector.tensor_scalar(weight[:, 0, :], den[:], 0.5, None, ALU.mult))
                step(nc.vector.tensor_tensor(weight[:, 1, :], weight[:, 0, :], gap[:], ALU.mult))

            def slot_map(p):
                dve.wait_ge(slots_ready, p + 1)
                with dve.Fori(0, TT // (2 * HOTS)) as i:
                    for at in range(2 * HOTS):
                        t, k = 2 * HOTS * i + at, at % HOTS
                        dve.wait_ge(slot_map_ps, p * TT + t + 1)
                        nc.vector.tensor_scalar(in_lane[:, k, 1, :], lane[:], slot_lane[:, 1, one(t)], None, ALU.is_equal)
                        for j in range(TOPK):
                            last = nc.vector.tensor_scalar(in_tile[:, k, j, :], tile_count[:], slot_tile[:, j, one(t)], None, ALU.is_equal)
                        last.then_inc(dve_hot, 1)
                step(nc.vector.tensor_tensor(past[:], tile_no[:], ends[:].unsqueeze(1).to_broadcast([P, NT, E]), ALU.is_ge))
                step(nc.vector.tensor_reduce(expert_f[:], past[:], AX.X, ALU.add))
                nc.vector.tensor_scalar(expert[:], expert_f[:], float(E - 1), None, ALU.min).then_inc(experts_known, 1)
                dve.wait_ge(slot_map_ps, (p + 1) * TT + HOTS)
                nc.vector.tensor_scalar(row_high[:], ps_slot_map[:, 1, :], float(P), None, ALU.mult)
                step(nc.vector.tensor_scalar(unused[:], ps_slot_map[:, 0, :], 0.0, None, ALU.is_equal))
                step(nc.vector.tensor_tensor(unused[:], unused[:], unused_no[:], ALU.mult))
                step(nc.vector.tensor_tensor(row_high[:], row_high[:], unused[:], ALU.add))
                step(nc.vector.tensor_tensor(row_f[:], ps_slot_map[:, 0, :], row_high[:], ALU.add))
                step(nc.vector.tensor_scalar(row_of[:], row_f[:], -1.0, None, ALU.add))
                nc.vector.tensor_scalar(token[:], row_of[:], TOKENS - 1, None, ALU.bitwise_and).then_inc(tokens_ready, 1)

            def turned(p, i, k):
                n, b = tile_of(p, i, k)
                dve.wait_ge(xsT_ps, done(n))
                dve.wait_ge(h_ps, done(n - 2))
                nc.vector.tensor_copy(xsT[:, b, :], ps_t[b][:, 0:P]).then_inc(xsT_sb, 1)

            def hidden(p, i, k):
                n, b = tile_of(p, i, k)
                dve.wait_ge(h_ps, done(n))
                dve.wait_ge(w_up_sb, done(n))
                dve.wait_ge(y_ps, done(n - 2))
                for c in range(HC // 2, HC):
                    last = nc.vector.tensor_scalar(hT[:, b, c, :], ps_h[b][c], w_up[:, k % AHEAD, B1_AT + c:B1_AT + c + 1],
                                                   0.0, ALU.add, ALU.max)
                last.then_inc(h_dve, 1)

            def result(p, i, k):
                n, b = tile_of(p, i, k)
                dve.wait_ge(y_ps, done(n))
                wait(dve, y_out[k], 16 * (uses_of(p, k) + i))
                nc.vector.tensor_tensor(ys[:, k, :], ps_y[b], w_up[:, k, B2_AT:B2_AT + D], ALU.add).then_inc(y_sb, 1)

            def combine():
                for t in range(TT):
                    b = t // BT
                    seq = rows[:, b % SEQS, t % BT, :, :]
                    if t % BT == 0:
                        dve.wait_ge(rows_in[b % SEQS], 16 * TOPK * (b // SEQS + 1 + (0 if b % SEQS else NB)))
                    step(nc.vector.scalar_tensor_tensor(x[:, t, :], seq[:, 0, :], weight[:, 0, t:t + 1], x[:, t, :],
                                                        ALU.mult, ALU.add))
                    nc.vector.scalar_tensor_tensor(x[:, t, :], seq[:, 1, :], weight[:, 1, t:t + 1], x[:, t, :],
                                                   ALU.mult, ALU.add).then_inc(combined, 1)

            def take_in(b, j):
                if j == 0:
                    dve.wait_ge(seq_combined, b + 1)
                    wait(dve, xb_ready, b)
                nc.vector.bn_stats(stats[:, j, :], x[:, one(BT * b + j), :].rearrange("p o d -> p (o d)")).then_inc(seq_stats, 1)

            def moments(b):
                wait_alone(dve, seq_stats, BT * (b + 1), dve_waited)
                for j in range(BT):
                    last = nc.vector.bn_aggr(meanvar[:, j, :], stats[:, j, :])
                step_counted(last, seq_meanvar, b + 1)
                nc.vector.tensor_scalar(var_eps[:, 0:BT], meanvar[:, 0:BT, 1], EPS, None, ALU.add).then_inc(var_ready, 1)

            def low(b, which):
                dve.wait_ge(qk_high, 2 * b + which + 1)
                parts = (q_parts, k_parts)[which]
                nc.vector.scalar_tensor_tensor(parts[:, 1, :], ps_spare, bqk[:, which:which + 1], parts[:, 0, :].bitcast(F32),
                                               ALU.add, ALU.subtract).then_inc(qk_low, 1)

            def v_done(b):
                dve.wait_ge(v_ps, b + 1)
                wait(dve, vx_ready, 4 * b)
                nc.vector.tensor_tensor(v_rows[:].rearrange("p t h d -> p t (h d)"), ps_spare.rearrange("p (t n) -> p t n", t=BT),
                                        bvo[:, 0:1, :].to_broadcast([P, BT, D]), ALU.add).then_inc(v_sb, 1)

            def maximum(b, g, j, c, banks=ps_s):
                block = 16 * (4 * b + g) + 4 * j + c
                dve.wait_ge(s_ps, block + 1)
                if j == 0 and c == 0:
                    wait(dve, maxT_ps, 4 * b + g - 1)
                nc.vector.tensor_reduce(neg_max[:, g % 2, j, c:c + 1], banks[c % len(banks)], AX.X, ALU.max, negate=True).then_inc(s_max, 1)

            def max_done(b, g):
                u = 4 * b + g
                dve.wait_ge(maxT_ps, u + 1)
                dve.wait_ge(max_high, u + 1)
                nc.vector.tensor_tensor(max_parts[:, 1, :], ps_spare[0:J, :], max_parts[:, 0, :].bitcast(F32),
                                        ALU.subtract).then_inc(max_sb, 1)

            def step_counted(ins, semaphore, count):
                ins.then_inc(semaphore, 1)
                dve.wait_ge(semaphore, count)

            def normalize(b, g):
                u = 4 * b + g
                acc = ps_spare.rearrange("p (t j r) -> p t j r", t=BT, j=J)
                dve.wait_ge(acc_turned, u + 1)
                step_counted(nc.vector.reciprocal(recip[:], acc[:, :, :, DEN]), recip_ready, u + 1)
                if g == 0:
                    wait(dve, attn_turned, b)
                nc.vector.tensor_tensor(attn[:, :, J * g:J * g + J, :], acc[:, :, :, 0:HD],
                                        recip[:].unsqueeze(3).to_broadcast([P, BT, J, HD]), ALU.mult).then_inc(attn_ready, 1)

            def out_done(b):
                dve.wait_ge(o_ps, b + 1)
                dve.wait_ge(bo_added, b + 1)
                xs4 = x[:, bass.ds(4 * b, BT), :]
                nc.vector.tensor_tensor(xs4, ps_spare.rearrange("p (t n) -> p t n", t=BT), xs4, ALU.add).then_inc(o_sb, 1)

            def attention():
                for j in range(BT):
                    take_in(0, j)
                moments(0)
                low(0, 0)
                low(0, 1)
                v_done(0)
                for j in range(BT):
                    take_in(1, j)
                moments(1)
                for u in range(2):
                    for j in range(J):
                        for c in range(BT):
                            maximum(0, u, j, c, ps_first)
                    if u == 0:
                        max_done(0, 0)

                def finish(b, g, what):
                    if what == "turn_max":
                        max_done(b + (g + 1) // G, (g + 1) % G)
                    elif what == "turn_acc":
                        normalize(b - (g == 0), (g - 1) % G)
                    elif what == "q":
                        low(b + 1, 0)
                    elif what == "k":
                        low(b + 1, 1)
                    elif what == "v":
                        v_done(b + 1)
                    elif what == "project":
                        out_done(b - 1)

                def run(b, first, after):
                    for g in range(G):
                        ahead = not (after == 0 and g >= 2)
                        for c in range(BT):
                            at = 4 * g + c - 1
                            if at >= 0:
                                finish(b, at // 4, tasks(at // 4, at % 4, first, after))
                            for i in range(BT):
                                if ahead:
                                    maximum(b + (g + 2) // G, (g + 2) % G, c, i)
                            if after == 0 and g == G - 1 and c < CHUNKS - 1:
                                dve.wait_ge(o_sb, NB - 1)
                                dve.wait_ge(xb_ready, NB)
                                statistics(c)
                            if after == 2 and (g, c) in STATISTICS:
                                take_in(b + 2, STATISTICS.index((g, c)))
                            if after == 2 and (g, c) == STATISTICS[-1]:
                                moments(b + 2)

                sequences(dve, run)
                normalize(NB - 1, G - 1)
                out_done(NB - 1)
                dve.wait_ge(o_sb, NB)

            for p in range(PHASES):
                if p == 1:
                    attention()
                front(p)
                route(p)
                slot_map(p)
                mix(p)
                turned(p, 0, 0)
                turned(p, 0, 1)
                hidden(p, 0, 0)

                def tile_step(i, k, up1, up2):
                    if up2:
                        turned(p, i, k + 2)
                    if up1:
                        hidden(p, i, k + 1)
                    result(p, i, k)

                tiles(dve, tile_step)
            combine()


def kernel(**inputs):
    import numpy as np
    import concourse.bacc as bacc
    from concourse.bass_utils import run_bass_kernel_spmd

    a = {k: np.asarray(v) for k, v in inputs.items()}
    w1, w2 = a["L0_ffn_W1"], a["L0_ffn_W2"]
    experts = np.concatenate([
        w1,
        a["L0_ffn_b1"].reshape(E, HC, P).transpose(0, 2, 1),
        np.broadcast_to(a["L0_ffn_b2"][:, None, :], (E, P, D)),
        w2.reshape(E, HC, P, D).transpose(0, 2, 1, 3).reshape(E, P, HC * D),
    ], axis=2)
    by_dim = np.arange(D).reshape(HEADS, HD).T.ravel()
    wqkv = np.stack([a["L0_attn_Wq"].T[:, by_dim], a["L0_attn_Wk"].T[:, by_dim], a["L0_attn_Wv"].T], axis=1)
    bqk = np.stack([a["L0_attn_bq"][by_dim], a["L0_attn_bk"][by_dim]], axis=1)
    bvo = np.stack([a["L0_attn_bv"], a["L0_attn_bo"]])
    attn = {"wqkv": wqkv, "wo": a["L0_attn_Wo"].T, "bqk": bqk, "bvo": bvo}
    arrays = {"x": a["L0_attn_x"].reshape(TOKENS, D), "wr": a["L0_ffn_Wr"], "br": a["L0_ffn_br"], "experts": experts, **attn}
    arrays = {k: np.ascontiguousarray(v) for k, v in arrays.items()}
    nc = bacc.Bacc("TRN2", target_bir_lowering=False, num_devices=1)
    t = {k: nc.dram_tensor("in_" + k, v.shape, F32, kind="ExternalInput").ap() for k, v in arrays.items()}
    out = nc.dram_tensor("out", (TOKENS, D), F32, kind="ExternalOutput").ap()
    build(nc, t["x"], t["wr"], t["br"], t["experts"], t["wqkv"], t["wo"], t["bqk"], t["bvo"], out)
    r = run_bass_kernel_spmd(nc, [{"in_" + k: v for k, v in arrays.items()}], core_ids=[0])
    return r.results[0]["out"].reshape(8, 512, D)
```
